# Optimizing a Trainium2 kernel written in Bass

```python
import numpy as np
import jax
import jax.numpy as jnp

def _softmax(x, axis=-1):
    return jax.nn.softmax(x, axis=axis)
def _gelu(x):
    return jax.nn.gelu(x, approximate=True)
def _silu(x):
    return jax.nn.silu(x)
def _sigmoid(x):
    return jax.nn.sigmoid(x)
def _layernorm(x, axis=-1, eps=1e-5):
    m = jnp.mean(x, axis=axis, keepdims=True)
    v = jnp.var(x, axis=axis, keepdims=True)
    return (x - m) / jnp.sqrt(v + eps)
def _scatter_add(tgt, idx, src, axis=0):
    return tgt.at[idx].add(src)
def _segment_sum(src, seg, n):
    return jax.ops.segment_sum(src, seg, n)

kernel_name = 'mk_conv_seq_d1_conv_nchw512_04e874'

def setup_inputs(seed: int = 0):
    np.random.seed(seed)
    _w = jnp.asarray
    def _rec_inputs():
        import jax
        import jax.numpy as jnp
        _gk = jax.random.key(seed)
        x = 7.22e-05 + 1 * jax.random.normal(jax.random.fold_in(_gk, 1), (16, 512, 32, 32), jnp.float32)
        return x
    x = _rec_inputs()
    def _L0_conv_setup():
        import jax, jax.numpy as jnp
        import numpy as np
        NUM_GROUPS = 32
        EPS = 1e-06

        def group_norm(x, gamma, beta):
            B, C, H, W = x.shape
            xg = x.reshape(B, NUM_GROUPS, C // NUM_GROUPS, H, W)
            mean = xg.mean(axis=(2, 3, 4), keepdims=True)
            var = xg.var(axis=(2, 3, 4), keepdims=True)
            xn = ((xg - mean) * jax.lax.rsqrt(var + EPS)).reshape(B, C, H, W)
            return xn * gamma[None, :, None, None] + beta[None, :, None, None]

        def conv1x1(x, w, b):
            return jnp.einsum('bchw,oc->bohw', x, w) + b[None, :, None, None]
        key = jax.random.key(seed)
        B, C, H, W = (16, 512, 32, 32)
        ks = jax.random.split(key, 12)
        s = 1.0 / np.sqrt(C)
        return {'x': jax.random.normal(ks[0], (B, C, H, W), dtype=jnp.float32), 'gn_gamma': jnp.ones((C,), dtype=jnp.float32), 'gn_beta': jnp.zeros((C,), dtype=jnp.float32), 'wq': jax.random.normal(ks[1], (C, C), dtype=jnp.float32) * s, 'bq': jnp.zeros((C,), dtype=jnp.float32), 'wk': jax.random.normal(ks[2], (C, C), dtype=jnp.float32) * s, 'bk': jnp.zeros((C,), dtype=jnp.float32), 'wv': jax.random.normal(ks[3], (C, C), dtype=jnp.float32) * s, 'bv': jnp.zeros((C,), dtype=jnp.float32), 'wp': jax.random.normal(ks[4], (C, C), dtype=jnp.float32) * s, 'bp': jnp.zeros((C,), dtype=jnp.float32)}
    _L0_conv_all = _L0_conv_setup()
    _L0_conv_in = {k: v for k, v in _L0_conv_all.items() if k in ('gn_gamma', 'gn_beta', 'wq', 'bq', 'wk', 'bk', 'wv', 'bv', 'wp', 'bp', )}
    del _L0_conv_all

    return {
        "x": x,
        "L0_conv_gn_gamma": _L0_conv_in["gn_gamma"],
        "L0_conv_gn_beta": _L0_conv_in["gn_beta"],
        "L0_conv_wq": _L0_conv_in["wq"],
        "L0_conv_bq": _L0_conv_in["bq"],
        "L0_conv_wk": _L0_conv_in["wk"],
        "L0_conv_bk": _L0_conv_in["bk"],
        "L0_conv_wv": _L0_conv_in["wv"],
        "L0_conv_bv": _L0_conv_in["bv"],
        "L0_conv_wp": _L0_conv_in["wp"],
        "L0_conv_bp": _L0_conv_in["bp"],
    }

def reference(x, L0_conv_gn_gamma, L0_conv_gn_beta, L0_conv_wq, L0_conv_bq, L0_conv_wk, L0_conv_bk, L0_conv_wv, L0_conv_bv, L0_conv_wp, L0_conv_bp):
    import jax
    import jax.numpy as jnp
    def _L0_conv_ref(x, gn_gamma, gn_beta, wq, bq, wk, bk, wv, bv, wp, bp):
        import jax, jax.numpy as jnp
        import numpy as np
        NUM_GROUPS = 32
        EPS = 1e-06

        def group_norm(x, gamma, beta):
            B, C, H, W = x.shape
            xg = x.reshape(B, NUM_GROUPS, C // NUM_GROUPS, H, W)
            mean = xg.mean(axis=(2, 3, 4), keepdims=True)
            var = xg.var(axis=(2, 3, 4), keepdims=True)
            xn = ((xg - mean) * jax.lax.rsqrt(var + EPS)).reshape(B, C, H, W)
            return xn * gamma[None, :, None, None] + beta[None, :, None, None]

        def conv1x1(x, w, b):
            return jnp.einsum('bchw,oc->bohw', x, w) + b[None, :, None, None]
        B, C, H, W = x.shape
        residual = x
        xn = group_norm(x, gn_gamma, gn_beta)
        q = conv1x1(xn, wq, bq).reshape(B, C, H * W)
        k = conv1x1(xn, wk, bk).reshape(B, C, H * W)
        v = conv1x1(xn, wv, bv).reshape(B, C, H * W)
        scale = C ** (-0.5)
        energy = jnp.einsum('bci,bcj->bij', q, k) * scale
        attn = jax.nn.softmax(energy, axis=-1)
        out = jnp.einsum('bij,bcj->bci', attn, v).reshape(B, C, H, W)
        out = conv1x1(out, wp, bp)
        return out + residual

    def _gn(v, G=32, eps=1e-5):
        B_, C_, H_, W_ = v.shape
        g = v.reshape(B_, G, C_ // G, H_, W_)
        m = jnp.mean(g, axis=(2, 3, 4), keepdims=True)
        s = jnp.var(g, axis=(2, 3, 4), keepdims=True)
        return ((g - m) / jnp.sqrt(s + eps)).reshape(v.shape)

    def _ln_c(v, eps=1e-6):
        m = jnp.mean(v, axis=1, keepdims=True)
        s = jnp.var(v, axis=1, keepdims=True)
        return (v - m) / jnp.sqrt(s + eps)

    def _ln_t(v, eps=1e-5):
        m = jnp.mean(v, axis=-1, keepdims=True)
        s = jnp.var(v, axis=-1, keepdims=True)
        return (v - m) / jnp.sqrt(s + eps)

    def _to_tokens(v):
        B_, C_, H_, W_ = v.shape
        return v.reshape(B_, C_, H_ * W_).transpose(0, 2, 1)
    def _from_tokens(t, like):
        B_, C_, H_, W_ = like.shape
        return t.transpose(0, 2, 1).reshape(B_, C_, H_, W_)

    x = _L0_conv_ref(x, L0_conv_gn_gamma, L0_conv_gn_beta, L0_conv_wq, L0_conv_bq, L0_conv_wk, L0_conv_bk, L0_conv_wv, L0_conv_bv, L0_conv_wp, L0_conv_bp)
    return x


_drawn_inputs = setup_inputs


def setup_inputs(seed=0):
    import zlib

    import numpy as np

    out = dict(_drawn_inputs(seed))
    spreads = {'L0_conv_gn_gamma': (1.0, 0.551),
     'L0_conv_gn_beta': (0.0, 0.1),
     'L0_conv_bq': (0.0, 0.8),
     'L0_conv_bk': (0.0, 0.8),
     'L0_conv_bv': (0.0, 0.1),
     'L0_conv_bp': (0.0, 0.1)}
    factors = {}
    for name, (base, spread) in spreads.items():
        noise = np.random.default_rng([zlib.crc32(name.encode()), seed]).standard_normal(out[name].shape)
        drawn = base * np.exp(spread * noise) if base else spread * noise
        out[name] = jnp.asarray(drawn.astype(out[name].dtype))
    for name, factor in factors.items():
        out[name] = (out[name] * factor).astype(out[name].dtype)
    return out
```

```python
from contextlib import ExitStack

import numpy as np
import concourse.bass as bass
from concourse import mybir

F32 = mybir.dt.float32
F32R = mybir.dt.float32r
ALU = mybir.AluOpType
ACT = mybir.ActivationFunctionType
AX = mybir.AxisListType

GAMMA, BETA, BQ, BK, BV, BP = range(6)


def build(nc, x, wq, wk, wv, wpt, vecs, out):
    B, C, N = x.shape
    P = 128
    KC = C // P
    NT = N // P
    HN = N // 2
    TH = NT // 2
    GROUP = C // 32
    EPS = 1e-6
    SCALE = float(C) ** -0.5
    BN_OUT = 6
    CONST_STEPS = 7
    BIAS_STEPS = 5

    def image_turns(has_next, has_next2):
        return ([("S1", 0), ("S2", 0)] * has_next + [("U", 1, g) for g in range(KC)] + [("O", 0, g) for g in range(KC)]
                + [("K", 0), ("K", 1)] * has_next + [("S1", 1), ("S2", 1)] * has_next2
                + [("U", 0, g) for g in range(KC)] * has_next + [("O", 1, g) for g in range(KC)]
                + [("V", j) for j in range(NT)] * has_next)

    TURNS = len(image_turns(True, True))
    first = ([("G", 0), ("G", 1), ("S1", 0, 0), ("G", 2), ("S2", 0, 0), ("G", 3), ("BQK",), ("S1", 0, 1), ("M", 0),
              ("S2", 0, 1), ("M", 1), ("M", 2), ("M", 3), ("BVP",)] + [("U", 0, g) for g in range(KC)]
             + [("K", 0), ("K", 1)] + [("V", 0), ("V", 1), ("V", 2), ("S1", 1, 0), ("V", 3), ("V", 4), ("V", 5),
                                       ("S2", 1, 0), ("V", 6), ("V", 7)])
    FIRST = {what: n for n, what in enumerate(first)}
    assert TURNS % 2 == 0 and len(first) == TURNS

    def turns(b, has_next=True, has_next2=True):
        start = TURNS * (b + 1)
        if isinstance(b, int) and b == B - 1:
            start += len(image_turns(True, False)) - TURNS
        table = {what: n for n, what in enumerate(image_turns(has_next, has_next2))}
        return lambda *what: (start + table[what], table[what] % 2)

    ctx = ExitStack()
    with ctx:
        def sb(name, shape, dt=F32):
            return ctx.enter_context(nc.sbuf_tensor(name, shape, dt))

        def sem(name):
            return ctx.enter_context(nc.semaphore(name))

        x_in = sb("x_in", [P, 2, N])
        xn_hi = [sb(f"xn_hi{p}", [P, KC, N], F32R) for p in range(2)]
        xn_lo = [sb(f"xn_lo{p}", [P, KC, N], F32R) for p in range(2)]
        u_hi = sb("u_hi", [P, KC, HN], F32R)
        u_lo = sb("u_lo", [P, KC, HN], F32R)
        prob = sb("prob", [P, 2, N])
        g_hi = sb("g_hi", [P, KC, C], F32R)
        g_lo = sb("g_lo", [P, KC, C], F32R)
        m_hi = sb("m_hi", [P, KC, C], F32R)
        m_lo = sb("m_lo", [P, KC, C], F32R)
        res = sb("res", [P, KC, HN])
        kdot = sb("kdot", [P, N])
        ident = sb("ident", [P, P])
        avg = sb("avg", [P, P])
        ones = sb("ones", [P, 1])
        vec = sb("vec", [P, 6, KC])
        u_bias = sb("u_bias", [P, KC])
        k_row = sb("k_row", [P, KC])
        o_bias = sb("o_bias", [P, KC])
        k_tmp = sb("k_tmp", [P, 2, KC])
        k_sum = sb("k_sum", [P, 2])
        k_const = sb("k_const", [P, 1])
        t_bias = sb("t_bias", [P, 2, NT])
        bn = sb("bn", [P, 2, 2 * BN_OUT])
        mv = sb("mv", [P, 2, 2])
        mean = sb("mean", [P, 2])
        dev = sb("dev", [P, 2])
        sq = sb("sq", [P, 2])
        ex = sb("ex", [P, 2])
        var_eps = sb("var_eps", [P, 2])
        half_neg = sb("half_neg", [P, 2])
        rstd = sb("rstd", [P, 2])
        gain = sb("gain", [P, 2])
        row_max = sb("row_max", [P, 2])
        neg_shift = sb("neg_shift", [P, 2])
        row_sum = sb("row_sum", [P, 2])
        row_inv = sb("row_inv", [P, 2])
        with ExitStack() as early:
            w_q, w_k, w_v, w_pt = [early.enter_context(nc.sbuf_tensor(n, [P, KC, C], F32))
                                   for n in ("w_q", "w_k", "w_v", "w_pt")]
        v_hi = sb("v_hi", [P, NT, C], F32R)
        v_lo = sb("v_lo", [P, NT, C], F32R)
        pt_hi = sb("pt_hi", [P, NT, HN], F32R)
        pt_lo = sb("pt_lo", [P, NT, HN], F32R)

        ps_e = ctx.enter_context(nc.psum_tensor("ps_e", [P, 2, N], F32))
        ps_t = ctx.enter_context(nc.psum_tensor("ps_t", [P, N], F32))
        ps_a = ctx.enter_context(nc.psum_tensor("ps_a", [P, 2, HN], F32))

        s_vec = sem("s_vec")
        s_wq, s_wk, s_wv, s_wpt = sem("s_wq"), sem("s_wk"), sem("s_wv"), sem("s_wpt")
        s_x = [sem(f"s_x{j}") for j in range(2)]
        s_res = [sem(f"s_res{g}") for g in range(KC)]
        s_out = [sem(f"s_out{g}") for g in range(KC)]
        s_const = sem("s_const")
        s_rstd = sem("s_rstd")
        s_acc = sem("s_acc")
        s_e = sem("s_e")
        s_t = sem("s_t")
        s_whi = sem("s_whi")
        s_xhi = sem("s_xhi")
        s_uhi = sem("s_uhi")
        s_vhi = sem("s_vhi")
        s_exp = sem("s_exp")
        s_pthi = sem("s_pthi")
        s_free = sem("s_free")
        s_bias = sem("s_bias")
        s_bn = sem("s_bn")
        s_mv = sem("s_mv")
        s_dev = sem("s_dev")
        s_sq = sem("s_sq")
        s_ex = sem("s_ex")
        s_gain = sem("s_gain")
        s_y = sem("s_y")
        s_xlo = sem("s_xlo")
        s_kdot = sem("s_kdot")
        s_max = sem("s_max")
        s_shift = sem("s_shift")
        s_inv = sem("s_inv")
        s_p = sem("s_p")
        s_ptlo = sem("s_ptlo")

        block = ctx.enter_context(nc.Block())

        def image_rows(ap, b, chunk, n0, n):
            return ap[bass.ds(b, 1), chunk * P:(chunk + 1) * P, n0:n0 + n].rearrange("a p i -> p (a i)")

        @block.sync
        def _(sp):
            def load_pair(b, pair):
                for j in range(2):
                    if not (isinstance(b, int) and b == 0 and pair == 0):
                        sp.wait_ge(s_kdot, KC * b + 2 * pair + j - 1)
                    sp.dma_start(x_in[:, j, :], image_rows(x, b, 2 * pair + j, 0, N)).then_inc(s_x[j], 16)

            def load_residual(b, h):
                for g in range(KC):
                    if not (isinstance(b, int) and b == 0 and h == 0):
                        sp.wait_ge(s_out[g], 16 * (2 * b + h))
                    sp.dma_start(res[:, g, :], image_rows(x, b, g, h * HN, HN)).then_inc(s_res[g], 16)

            def store(b, h, at):
                for g in range(KC):
                    sp.wait_ge(s_free, at("O", h, g)[0] + 1)
                    sp.dma_start(image_rows(out, b, g, h * HN, HN), res[:, g, :]).then_inc(s_out[g], 16)

            def body(b, has_next, has_next2):
                at = turns(b, has_next, has_next2)
                store(b, 0, at)
                if has_next2:
                    load_pair(b + 2, 0)
                load_residual(b, 1)
                store(b, 1, at)
                if has_next2:
                    load_pair(b + 2, 1)
                if has_next:
                    load_residual(b + 1, 0)

            sp.dma_start(vec[:], vecs).then_inc(s_vec, 16)
            sp.dma_start(w_q[:], wq.rearrange("(k p) c -> p k c", p=P)).then_inc(s_wq, 16)
            load_pair(0, 0)
            load_pair(0, 1)
            load_residual(0, 0)
            load_pair(1, 0)
            load_pair(1, 1)
            with nc.sync.Fori(0, B // 2 - 1) as i:
                for p in range(2):
                    body(2 * i + p, True, True)
            body(B - 2, True, False)
            body(B - 1, False, False)
            for g in range(KC):
                sp.wait_ge(s_out[g], 16 * 2 * B)

        @block.gpsimd
        def _(pool):
            s_step = s_const
            nc.gpsimd.memset(ident[:], 0.0).then_inc(s_step, 1)
            nc.gpsimd.memset(avg[:], 1.0 / GROUP).then_inc(s_step, 1)
            nc.gpsimd.memset(ones[:], 1.0).then_inc(s_step, 1)
            nc.gpsimd.memset(half_neg[:], -0.5).then_inc(s_step, 1)
            pool.wait_ge(s_step, 4)
            nc.gpsimd.affine_select(out=ident[:], in_=ident[:], compare_op=ALU.not_equal, fill=1.0, base=0,
                                    pattern=[[-1, P]], channel_multiplier=1).then_inc(s_step, 1)
            blocks = avg[:].rearrange("p (g c) -> p g c", c=GROUP)
            nc.gpsimd.affine_select(out=blocks, in_=blocks, compare_op=ALU.is_ge, fill=0.0, base=0,
                                    pattern=[[-GROUP, P // GROUP], [0, GROUP]], channel_multiplier=1).then_inc(s_step, 1)
            pool.wait_ge(s_step, 6)
            nc.gpsimd.affine_select(out=blocks, in_=blocks, compare_op=ALU.is_ge, fill=0.0, base=GROUP - 1,
                                    pattern=[[GROUP, P // GROUP], [0, GROUP]], channel_multiplier=-1).then_inc(s_step, 1)

            def root(at):
                pool.wait_ge(s_free, at + 1)
                nc.gpsimd.tensor_tensor(rstd[:], var_eps[:], half_neg[:], ALU.pow).then_inc(s_rstd, 1)

            root(FIRST[("S2", 0, 0)])
            root(FIRST[("S2", 0, 1)])
            root(FIRST[("S2", 1, 0)])
            with nc.gpsimd.Fori(0, B // 2 - 1) as i:
                for p in range(2):
                    root(turns(2 * i + p)("S2", 0)[0])
                    root(turns(2 * i + p)("S2", 1)[0])
            root(turns(B - 2, True, False)("S2", 0)[0])

        @block.tensor
        def _(pe):
            def product(acc, left_hi, left_lo, right_hi, right_lo, n, inc):
                for k in range(n):
                    nc.tensor.matmul(acc, left_hi(k), right_hi(k), start=(k == 0), stop=False)
                    nc.tensor.matmul(acc, left_hi(k), right_lo(k), start=False, stop=False)
                    last = nc.tensor.matmul(acc, left_lo(k), right_hi(k), start=False, stop=(k == n - 1))
                last.then_inc(inc, 1)

            def bank(index):
                return ps_a[:, index % 2, :]

            def u_turn(b, p, h, g, at, index):
                pe.wait_ge(s_xlo, KC * b + KC)
                pe.wait_ge(s_free, at - 1)
                cols = slice(g * P, (g + 1) * P)
                pix = slice(h * HN, (h + 1) * HN)
                product(bank(index), lambda k: g_hi[:, k, cols], lambda k: g_lo[:, k, cols],
                        lambda k: xn_hi[p][:, k, pix], lambda k: xn_lo[p][:, k, pix], KC, s_acc)

            def v_turn(p, j, at, index):
                pe.wait_ge(s_free, at - 1)
                pix = slice(j * P, (j + 1) * P)
                product(bank(index), lambda k: xn_hi[p][:, k, pix], lambda k: xn_lo[p][:, k, pix],
                        lambda k: m_hi[:, k, :], lambda k: m_lo[:, k, :], KC, s_acc)

            def o_turn(b, h, g, at, index):
                pe.wait_ge(s_ptlo, NT * b + TH * h + TH)
                pe.wait_ge(s_free, at - 1)
                cols = slice(g * P, (g + 1) * P)
                product(bank(index), lambda j: v_hi[:, j, cols], lambda j: v_lo[:, j, cols],
                        lambda j: pt_hi[:, j, :], lambda j: pt_lo[:, j, :], NT, s_acc)

            def k_turn(b, half, at, index):
                pe.wait_ge(s_kdot, KC * b + KC)
                pe.wait_ge(s_free, at - 1)
                for t in range(TH):
                    tile = (half * TH + t) * P
                    last = nc.tensor.matmul(bank(index)[:, t:t + 1], kdot[:, tile:tile + P], ones[:], start=True, stop=True)
                last.then_inc(s_acc, 1)

            def average(src, waited, count, at, index):
                pe.wait_ge(waited, count)
                if not isinstance(at, int) or at >= 2:
                    pe.wait_ge(s_free, at - 1)
                nc.tensor.matmul(bank(index)[:, 0:2], avg[:], src, start=True, stop=True).then_inc(s_acc, 1)

            def scores(b, p, t):
                tile = slice(t % TH * P, (t % TH + 1) * P)
                for k in range(KC):
                    for left, right, start, stop in ((u_hi, xn_hi[p], k == 0, False), (u_hi, xn_lo[p], False, False),
                                                     (u_lo, xn_hi[p], False, k == KC - 1)):
                        for jh in range(2):
                            pix = slice(jh * HN, (jh + 1) * HN)
                            last = nc.tensor.matmul(ps_e[:, t % 2, pix], left[:, k, tile], right[:, k, pix],
                                                    start=start, stop=stop)
                last.then_inc(s_e, 1)

            def transposes(b, t):
                pe.wait_ge(s_p, NT * b + t + 1)
                if t % TH:
                    pe.wait_ge(s_ptlo, NT * b + t)
                for j in range(NT):
                    cols = slice(j * P, (j + 1) * P)
                    last = nc.tensor.transpose(ps_t[:, cols], prob[:, t % 2, cols], ident[:])
                last.then_inc(s_t, 1)

            def body(b, p, has_next, has_next2):
                at = turns(b, has_next, has_next2)
                scores(b, p, 0)
                scores(b, p, 1)
                transposes(b, 0)
                scores(b, p, 2)
                transposes(b, 1)
                if has_next:
                    average(mv[:, :, 0], s_mv, 2 * b + 4, *at("S1", 0))
                scores(b, p, 3)
                transposes(b, 2)
                if has_next:
                    average(ex[:], s_ex, 2 * b + 4, *at("S2", 0))
                for g in range(KC):
                    u_turn(b, p, 1, g, *at("U", 1, g))
                    if g == KC - 2:
                        transposes(b, 3)
                for g in range(KC):
                    o_turn(b, 0, g, *at("O", 0, g))
                scores(b, p, 4)
                scores(b, p, 5)
                transposes(b, 4)
                if has_next:
                    k_turn(b + 1, 0, *at("K", 0))
                    k_turn(b + 1, 1, *at("K", 1))
                scores(b, p, 6)
                transposes(b, 5)
                if has_next2:
                    average(mv[:, :, 0], s_mv, 2 * b + 5, *at("S1", 1))
                scores(b, p, 7)
                transposes(b, 6)
                if has_next2:
                    average(ex[:], s_ex, 2 * b + 5, *at("S2", 1))
                for g in range(KC):
                    if has_next:
                        u_turn(b + 1, 1 - p, 0, g, *at("U", 0, g))
                    if g == KC - 2:
                        transposes(b, 7)
                for g in range(KC):
                    o_turn(b, 1, g, *at("O", 1, g))
                if has_next:
                    for j in range(NT):
                        v_turn(1 - p, j, *at("V", j))

            def weight_product(left, right, g, index):
                if index >= 2:
                    pe.wait_ge(s_free, index - 1)
                for k in range(KC):
                    last = nc.tensor.matmul(bank(index), left[:, k, g * P:(g + 1) * P], right[:, k, :],
                                            start=(k == 0), stop=(k == KC - 1))
                last.then_inc(s_acc, 1)

            def column_products(index, which):
                pe.wait_ge(s_free, index - 1)
                for n, (left, column) in enumerate(which):
                    for g in range(KC):
                        for k in range(KC):
                            last = nc.tensor.matmul(bank(index)[:, n * KC + g:n * KC + g + 1],
                                                    left[:, k, g * P:(g + 1) * P], vec[:, column, k:k + 1],
                                                    start=(k == 0), stop=(k == KC - 1))
                last.then_inc(s_acc, 1)

            pe.wait_ge(s_const, CONST_STEPS)
            pe.wait_ge(s_vec, 16)
            pe.wait_ge(s_wq, 16)
            pe.wait_ge(s_wk, 16)
            for index, what in enumerate(first):
                if what[0] == "G":
                    weight_product(w_q, w_k, what[1], index)
                elif what[0] == "BQK":
                    column_products(index, ((w_k, BQ), (w_q, BK)))
                elif what[0] == "M":
                    if what[1] == 0:
                        pe.wait_ge(s_wv, 16)
                        pe.wait_ge(s_wpt, 16)
                    weight_product(w_v, w_pt, what[1], index)
                elif what[0] == "BVP":
                    column_products(index, ((w_pt, BV),))
                elif what[0] == "S1":
                    average(mv[:, :, 0], s_mv, 2 * what[1] + what[2] + 1, index, index)
                elif what[0] == "S2":
                    average(ex[:], s_ex, 2 * what[1] + what[2] + 1, index, index)
                elif what[0] == "U":
                    u_turn(0, 0, 0, what[2], index, index)
                elif what[0] == "K":
                    k_turn(0, what[1], index, index)
                elif what[0] == "V":
                    v_turn(0, what[1], index, index)
            with nc.tensor.Fori(0, B // 2 - 1) as i:
                for p in range(2):
                    body(2 * i + p, p, True, True)
            body(B - 2, 0, True, False)
            body(B - 1, 1, False, False)

        @block.scalar
        def _(act):
            def split_x(b, p, chunk):
                act.wait_ge(s_y, KC * b + chunk + 1)
                nc.scalar.activation(xn_hi[p][:, chunk, :], x_in[:, chunk % 2, :], ACT.Identity,
                                     bias=vec[:, BETA, chunk:chunk + 1]).then_inc(s_xhi, 1)

            def split_u(g, at, index):
                act.wait_ge(s_acc, at + 1)
                nc.scalar.activation(u_hi[:, g, :], ps_a[:, index % 2, :], ACT.Identity,
                                     bias=u_bias[:, g:g + 1]).then_inc(s_uhi, 1)

            def split_v(j, at, index):
                act.wait_ge(s_acc, at + 1)
                nc.scalar.activation(v_hi[:, j, :], ps_a[:, index % 2, :], ACT.Copy).then_inc(s_vhi, 1)

            def exponent(b, t):
                act.wait_ge(s_shift, NT * b + t + 1)
                nc.scalar.activation(prob[:, t % 2, :], ps_e[:, t % 2, :], ACT.Exp, bias=neg_shift[:, t % 2:t % 2 + 1],
                                     accum_out=row_sum[:, t % 2:t % 2 + 1]).then_inc(s_exp, 1)

            def split_pt(b, t):
                act.wait_ge(s_t, NT * b + t + 1)
                cols = slice(t % TH * P, (t % TH + 1) * P)
                nc.scalar.activation(pt_hi[:, :, cols], ps_t[:].rearrange("p (j i) -> p j i", i=P),
                                     ACT.Copy).then_inc(s_pthi, 1)

            def half(b, h, at, u_half, u_turns, chunks):
                for t in range(TH * h, TH * h + TH):
                    if t % TH:
                        split_pt(b, t - 1)
                    exponent(b, t)
                for g in range(KC):
                    if u_turns:
                        split_u(g, *at("U", u_half, g))
                    if g == KC - 2:
                        split_pt(b, TH * h + TH - 1)
                for bx, px, chunk in chunks:
                    split_x(bx, px, chunk)

            def body(b, p, has_next, has_next2):
                at = turns(b, has_next, has_next2)
                half(b, 0, at, 1, True, [(b + 1, 1 - p, c) for c in (2, 3)] if has_next else [])
                half(b, 1, at, 0, has_next, [(b + 2, p, c) for c in (0, 1)] if has_next2 else [])
                if has_next:
                    for j in range(NT):
                        split_v(j, *at("V", j))

            act.dma_start(w_k[:], wk.rearrange("(k p) c -> p k c", p=P)).then_inc(s_wk, 16)
            act.dma_start(w_v[:], wv.rearrange("(k p) c -> p k c", p=P)).then_inc(s_wv, 16)
            act.dma_start(w_pt[:], wpt.rearrange("(k p) c -> p k c", p=P)).then_inc(s_wpt, 16)
            act.wait_ge(s_vec, 16)
            for index, what in enumerate(first):
                if what[0] in "GM":
                    act.wait_ge(s_acc, index + 1)
                    dst, scale = (g_hi, SCALE) if what[0] == "G" else (m_hi, 1.0)
                    nc.scalar.activation(dst[:, what[1], :], ps_a[:, index % 2, :], ACT.Copy,
                                         scale=scale).then_inc(s_whi, 1)
                if what[0] == "BQK":
                    split_x(0, 0, 0)
                    split_x(0, 0, 1)
                if what[0] == "BVP":
                    split_x(0, 0, 2)
                    split_x(0, 0, 3)
                if what[0] == "U":
                    if what[2] == 0:
                        act.wait_ge(s_bias, BIAS_STEPS)
                    split_u(what[2], index, index)
                if what[0] == "V":
                    split_v(what[1], index, index)
            split_x(1, 1, 0)
            split_x(1, 1, 1)
            with nc.scalar.Fori(0, B // 2 - 1) as i:
                for p in range(2):
                    body(2 * i + p, p, True, True)
            body(B - 2, 0, True, False)
            body(B - 1, 1, False, False)

        @block.vector
        def _(dve):
            def moments(b, pair, j):
                dve.wait_ge(s_x[j], 16 * (2 * b + pair + 1))
                for n in range(2):
                    last = nc.vector.bn_stats(bn[:, j, n * BN_OUT:(n + 1) * BN_OUT], x_in[:, j, n * HN:(n + 1) * HN])
                last.then_inc(s_bn, 1)

            def moments_done(b, pair):
                dve.wait_ge(s_bn, 2 * (2 * b + pair) + 2)

            def aggregate():
                for j in range(2):
                    last = nc.vector.bn_aggr(mv[:, j, :], bn[:, j, :])
                last.then_inc(s_mv, 1)

            def spread(b, pair, at, index):
                q = 2 * b + pair
                dve.wait_ge(s_acc, at + 1)
                nc.vector.tensor_tensor(dev[:], mv[:, :, 0], ps_a[:, index % 2, 0:2], ALU.subtract).then_inc(s_dev, 1)
                nc.vector.tensor_copy(mean[:], ps_a[:, index % 2, 0:2]).then_inc(s_free, 1)
                dve.wait_ge(s_dev, q + 1)
                nc.vector.tensor_tensor(sq[:], dev[:], dev[:], ALU.mult).then_inc(s_sq, 1)
                dve.wait_ge(s_sq, q + 1)
                nc.vector.tensor_tensor(ex[:], sq[:], mv[:, :, 1], ALU.add).then_inc(s_ex, 1)

            def variance(at, index):
                dve.wait_ge(s_acc, at + 1)
                nc.vector.tensor_scalar(var_eps[:], ps_a[:, index % 2, 0:2], EPS, None, ALU.add).then_inc(s_free, 1)

            def centre(b, pair):
                q = 2 * b + pair
                dve.wait_ge(s_rstd, q + 1)
                nc.vector.tensor_tensor(gain[:], rstd[:], vec[:, GAMMA, 2 * pair:2 * pair + 2],
                                        ALU.mult).then_inc(s_gain, 1)
                dve.wait_ge(s_gain, q + 1)
                for j in range(2):
                    nc.vector.tensor_scalar(x_in[:, j, :], x_in[:, j, :], mean[:, j:j + 1], gain[:, j:j + 1],
                                            ALU.subtract, ALU.mult).then_inc(s_y, 1)

            def split_x(b, p, chunk):
                dve.wait_ge(s_xhi, KC * b + chunk + 1)
                nc.vector.scalar_tensor_tensor(out=xn_lo[p][:, chunk, :], in0=x_in[:, chunk % 2, :],
                                               scalar=vec[:, BETA, chunk:chunk + 1],
                                               in1=xn_hi[p][:, chunk, :].bitcast(F32), op0=ALU.add,
                                               op1=ALU.subtract).then_inc(s_xlo, 1)

            def add_kdot(b, chunk):
                if chunk == 0:
                    nc.vector.tensor_scalar(kdot[:], x_in[:, 0, :], k_row[:, 0:1], k_const[:],
                                            ALU.mult, ALU.add).then_inc(s_kdot, 1)
                else:
                    dve.wait_ge(s_kdot, KC * b + chunk)
                    nc.vector.scalar_tensor_tensor(out=kdot[:], in0=x_in[:, chunk % 2, :],
                                                   scalar=k_row[:, chunk:chunk + 1], in1=kdot[:], op0=ALU.mult,
                                                   op1=ALU.add).then_inc(s_kdot, 1)

            def key_bias(p, half, at, index):
                dve.wait_ge(s_acc, at + 1)
                nc.vector.tensor_copy(t_bias[:, p, half * TH:(half + 1) * TH],
                                      ps_a[:, index % 2, 0:TH]).then_inc(s_free, 1)

            def split_u(b, h, g, index):
                dve.wait_ge(s_uhi, 2 * KC * b + KC * h + g + 1)
                nc.vector.scalar_tensor_tensor(out=u_lo[:, g, :], in0=ps_a[:, index % 2, :], scalar=u_bias[:, g:g + 1],
                                               in1=u_hi[:, g, :].bitcast(F32), op0=ALU.add,
                                               op1=ALU.subtract).then_inc(s_free, 1)

            def split_v(b, j, index):
                dve.wait_ge(s_vhi, NT * b + j + 1)
                nc.vector.tensor_tensor(v_lo[:, j, :], ps_a[:, index % 2, :], v_hi[:, j, :].bitcast(F32),
                                        ALU.subtract).then_inc(s_free, 1)

            def shift(b, p, t):
                dve.wait_ge(s_e, NT * b + t + 1)
                nc.vector.tensor_reduce(row_max[:, t % 2:t % 2 + 1], ps_e[:, t % 2, :], AX.X, ALU.max).then_inc(s_max, 1)
                dve.wait_ge(s_max, NT * b + t + 1)
                nc.vector.scalar_tensor_tensor(out=neg_shift[:, t % 2:t % 2 + 1], in0=row_max[:, t % 2:t % 2 + 1],
                                               scalar=t_bias[:, p, t:t + 1], in1=t_bias[:, p, t:t + 1], op0=ALU.add,
                                               op1=ALU.subtract, reverse1=True).then_inc(s_shift, 1)

            def normalise(b, t):
                dve.wait_ge(s_exp, NT * b + t + 1)
                nc.vector.reciprocal(row_inv[:, t % 2:t % 2 + 1], row_sum[:, t % 2:t % 2 + 1]).then_inc(s_inv, 1)
                dve.wait_ge(s_inv, NT * b + t + 1)
                nc.vector.tensor_scalar(prob[:, t % 2, :], prob[:, t % 2, :], row_inv[:, t % 2:t % 2 + 1], None,
                                        ALU.mult).then_inc(s_p, 1)

            def split_pt(b, t):
                dve.wait_ge(s_pthi, NT * b + t + 1)
                cols = slice(t % TH * P, (t % TH + 1) * P)
                nc.vector.tensor_tensor(pt_lo[:, :, cols], ps_t[:].rearrange("p (j i) -> p j i", i=P),
                                        pt_hi[:, :, cols].bitcast(F32), ALU.subtract).then_inc(s_ptlo, 1)

            def result(b, h, g, at, index):
                dve.wait_ge(s_acc, at + 1)
                dve.wait_ge(s_res[g], 16 * (2 * b + h + 1))
                nc.vector.scalar_tensor_tensor(out=res[:, g, :], in0=ps_a[:, index % 2, :], scalar=o_bias[:, g:g + 1],
                                               in1=res[:, g, :], op0=ALU.add, op1=ALU.add).then_inc(s_free, 1)

            def half(b, p, h, at, stats, u_of, keys):
                for n in range(TH):
                    t = TH * h + n
                    shift(b, p, t)
                    if n:
                        split_pt(b, t - 1)
                    if stats and n < 2:
                        moments(*stats, n)
                    if stats and n == 1:
                        moments_done(*stats)
                    normalise(b, t)
                    if stats and n == 1:
                        aggregate()
                    if keys and n == 1:
                        for k in range(2):
                            key_bias(1 - p, k, *at("K", k))
                    if stats and n == 2:
                        spread(*stats, *at("S1", h))
                    if stats and n == 3:
                        variance(*at("S2", h))
                for g in range(KC):
                    if u_of:
                        split_u(*u_of, g, at("U", 1 - h, g)[1])
                    if g == KC - 2:
                        split_pt(b, TH * h + TH - 1)
                if stats:
                    bs, pair = stats
                    ps = (1 - p) if h == 0 else p
                    centre(bs, pair)
                    split_x(bs, ps, 2 * pair)
                for g in range(KC):
                    result(b, h, g, *at("O", h, g))
                    if stats and g == 0:
                        add_kdot(bs, 2 * pair)
                        split_x(bs, ps, 2 * pair + 1)
                    if stats and g == 1:
                        add_kdot(bs, 2 * pair + 1)

            def body(b, p, has_next, has_next2):
                at = turns(b, has_next, has_next2)
                half(b, p, 0, at, (b + 1, 1) if has_next else None, (b, 1), False)
                half(b, p, 1, at, (b + 2, 0) if has_next2 else None, (b + 1, 0) if has_next else None, has_next)
                if has_next:
                    for j in range(NT):
                        split_v(b + 1, j, at("V", j)[1])

            def bias_done(n):
                dve.wait_ge(s_bias, n)

            dve.wait_ge(s_vec, 16)
            for j in range(2):
                moments(0, 0, j)
            moments_done(0, 0)
            aggregate()
            for index, what in enumerate(first):
                if what[0] in "GM":
                    n = what[1] + (KC if what[0] == "M" else 0)
                    dve.wait_ge(s_whi, n + 1)
                    hi, lo, scale = (g_hi, g_lo, SCALE) if what[0] == "G" else (m_hi, m_lo, 1.0)
                    nc.vector.scalar_tensor_tensor(out=lo[:, what[1], :], in0=ps_a[:, index % 2, :], scalar=scale,
                                                   in1=hi[:, what[1], :].bitcast(F32), op0=ALU.mult,
                                                   op1=ALU.subtract).then_inc(s_free, 1)
                elif what[0] == "S1":
                    spread(what[1], what[2], index, index)
                elif what[0] == "S2":
                    variance(index, index)
                elif what[0] == "BQK":
                    dve.wait_ge(s_acc, index + 1)
                    nc.vector.tensor_scalar(u_bias[:], ps_a[:, index % 2, 0:KC], SCALE, None, ALU.mult).then_inc(s_bias, 1)
                    nc.vector.tensor_scalar(k_row[:], ps_a[:, index % 2, KC:2 * KC], SCALE, None,
                                            ALU.mult).then_inc(s_free, 1)
                    nc.vector.tensor_tensor(k_tmp[:, 0, :], vec[:, BQ, :], vec[:, BK, :], ALU.mult).then_inc(s_bias, 1)
                    dve.wait_ge(s_free, index + 1)
                    nc.vector.tensor_tensor(k_tmp[:, 1, :], k_row[:], vec[:, BETA, :], ALU.mult).then_inc(s_bias, 1)
                    bias_done(3)
                    nc.vector.tensor_reduce(k_sum[:], k_tmp[:], AX.X, ALU.add).then_inc(s_bias, 1)
                    bias_done(4)
                    nc.vector.scalar_tensor_tensor(out=k_const[:], in0=k_sum[:, 0:1], scalar=SCALE, in1=k_sum[:, 1:2],
                                                   op0=ALU.mult, op1=ALU.add).then_inc(s_bias, 1)
                    centre(0, 0)
                    split_x(0, 0, 0)
                    bias_done(5)
                    add_kdot(0, 0)
                    split_x(0, 0, 1)
                    add_kdot(0, 1)
                    for j in range(2):
                        moments(0, 1, j)
                    moments_done(0, 1)
                    aggregate()
                elif what[0] == "BVP":
                    dve.wait_ge(s_acc, index + 1)
                    nc.vector.tensor_tensor(o_bias[:], ps_a[:, index % 2, 0:KC], vec[:, BP, :], ALU.add).then_inc(s_free, 1)
                    centre(0, 1)
                    for j in range(2):
                        split_x(0, 0, 2 + j)
                        add_kdot(0, 2 + j)
                elif what[0] == "U":
                    split_u(0, 0, what[2], index)
                elif what[0] == "K":
                    key_bias(0, what[1], index, index)
                    if what[1] == 1:
                        for j in range(2):
                            moments(1, 0, j)
                        moments_done(1, 0)
                        aggregate()
                elif what[0] == "V":
                    split_v(0, what[1], index)
            centre(1, 0)
            for j in range(2):
                split_x(1, 1, j)
                add_kdot(1, j)
            with nc.vector.Fori(0, B // 2 - 1) as i:
                for p in range(2):
                    body(2 * i + p, p, True, True)
            body(B - 2, 0, True, False)
            body(B - 1, 1, False, False)


def kernel(**inputs):
    import concourse.bacc as bacc
    from concourse.bass_utils import run_bass_kernel_spmd

    x = np.ascontiguousarray(inputs["x"])
    b, c, h, w = x.shape
    names = ("gn_gamma", "gn_beta", "bq", "bk", "bv", "bp")
    columns = [np.asarray(inputs["L0_conv_" + n]).reshape(-1, 128).T for n in names]
    arrays = {
        "x": x.reshape(b, c, h * w),
        "wq": np.ascontiguousarray(inputs["L0_conv_wq"]),
        "wk": np.ascontiguousarray(inputs["L0_conv_wk"]),
        "wv": np.ascontiguousarray(inputs["L0_conv_wv"]),
        "wp_t": np.ascontiguousarray(np.asarray(inputs["L0_conv_wp"]).T),
        "vecs": np.ascontiguousarray(np.stack(columns, axis=1)),
    }
    nc = bacc.Bacc("TRN2", target_bir_lowering=False, num_devices=1)
    args = [nc.dram_tensor(n, a.shape, mybir.dt.from_np(a.dtype), kind="ExternalInput").ap() for n, a in arrays.items()]
    out = nc.dram_tensor("out", (b, c, h * w), F32, kind="ExternalOutput").ap()
    build(nc, *args, out)
    result = run_bass_kernel_spmd(nc, [arrays], core_ids=[0])
    return result.results[0]["out"].reshape(b, c, h, w)
```

```python
from contextlib import ExitStack

import numpy as np
import concourse.bass as bass
from concourse import mybir

F32 = mybir.dt.float32
F32R = mybir.dt.float32r
ALU = mybir.AluOpType
ACT = mybir.ActivationFunctionType
AX = mybir.AxisListType

GAMMA, BETA, BQ, BK, BV, BP = range(6)


def build(nc, x, wq, wk, wv, wpt, vecs, scratch, out):
    B, C, N = x.shape
    P = 128
    KC = C // P
    NT = N // P
    HN = N // 2
    TH = NT // 2
    GROUP = C // 32
    EPS = 1e-6
    SCALE = float(C) ** -0.5
    BN_OUT = 6
    Q = 32
    NQ = P // Q
    CONST_STEPS = 15
    BANKS = 4

    def image_turns(has_next, has_next2):
        return ([("U", 1, 0), ("U", 1, 1)] + [("S1", 0)] * has_next + [("U", 1, 2), ("U", 1, 3)] + [("S2", 0)] * has_next
                + [("O", 0, g) for g in range(KC)]
                + [("U", 0, 0), ("U", 0, 1)] * has_next + [("S1", 1)] * has_next2 + [("U", 0, 2), ("U", 0, 3)] * has_next
                + [("S2", 1)] * has_next2 + [("O", 1, g) for g in range(KC)] + [("V", j) for j in range(NT)] * has_next)

    TURNS = len(image_turns(True, True))
    FIRST = {what: n for n, what in enumerate(
        [("G", 0), ("G", 1), ("G", 2), ("S1", 0), ("G", 3), ("S2", 0)] + [("M", g) for g in range(KC)]
        + [("U", g) for g in range(KC)] + [("V", 0), ("V", 1), ("V", 2), ("S1", 1), ("V", 3), ("V", 4), ("V", 5),
                                           ("S2", 1), ("V", 6), ("V", 7)])}
    assert TURNS % BANKS == 0 and len(FIRST) % BANKS == 0

    def turns(b, has_next=True, has_next2=True):
        start, shift = len(FIRST) + TURNS * b, 0
        if isinstance(b, int) and b == B - 1:
            shift = len(image_turns(True, False)) - TURNS
        table = {what: n for n, what in enumerate(image_turns(has_next, has_next2))}
        return lambda *what: (start + shift + table[what], (shift + table[what]) % BANKS)

    def early_turn(*what):
        return FIRST[what], FIRST[what] % BANKS

    def set_of(b, pair):
        return 2 * b + pair - 1

    ctx = ExitStack()
    with ctx:
        def sb(name, shape, dt=F32):
            return ctx.enter_context(nc.sbuf_tensor(name, shape, dt))

        def sem(name):
            return ctx.enter_context(nc.semaphore(name))

        x_in = sb("x_in", [P, 2, N])
        xn_hi = [sb(f"xn_hi{p}", [P, KC, N], F32R) for p in range(2)]
        xn_lo = [sb(f"xn_lo{p}", [P, KC, N], F32R) for p in range(2)]
        u_hi = sb("u_hi", [P, KC, HN], F32R)
        u_lo = sb("u_lo", [P, KC, HN], F32R)
        prob = sb("prob", [P, N])
        blocks_out = sb("blocks_out", [P, NQ, NT, Q])
        blocks_in = sb("blocks_in", [P, NQ, NT, Q])
        g_hi = sb("g_hi", [P, KC, C], F32R)
        g_lo = sb("g_lo", [P, KC, C], F32R)
        m_hi = sb("m_hi", [P, KC, C], F32R)
        m_lo = sb("m_lo", [P, KC, C], F32R)
        res = sb("res", [P, 2, HN])
        kdot = sb("kdot", [P, N])
        kdot_q = sb("kdot_q", [P, N // Q])
        col_hi = sb("col_hi", [P, N // Q], F32R)
        col_lo = sb("col_lo", [P, N // Q], F32R)
        avg = sb("avg", [P, P], F32R)
        same = sb("same", [P, P], F32R)
        vec = sb("vec", [P, 6, KC])
        u_bias = sb("u_bias", [P, KC])
        k_row = sb("k_row", [P, KC])
        o_bias = sb("o_bias", [P, KC])
        k_tmp = sb("k_tmp", [P, 2, KC])
        k_sum = sb("k_sum", [P, 2])
        k_const = sb("k_const", [P, 1])
        columns = sb("columns", [P, 2, KC])
        t_bias = sb("t_bias", [P, 2, NT])
        bn = sb("bn", [P, KC, 2 * BN_OUT])
        mv = sb("mv", [P, KC, 2])
        mom = sb("mom", [P, 2 * KC], F32R)
        mean = sb("mean", [P, KC])
        dev = sb("dev", [P, KC])
        sq = sb("sq", [P, KC])
        ex = sb("ex", [P, KC])
        var = sb("var", [P, KC])
        var_eps = sb("var_eps", [P, KC])
        eps = sb("eps", [P, KC])
        half_neg = sb("half_neg", [P, KC])
        rstd = sb("rstd", [P, KC])
        gain = sb("gain", [P, KC])
        row_max = sb("row_max", [P, 2])
        neg_shift = sb("neg_shift", [P, 2])
        row_sum = sb("row_sum", [P, 2])
        row_inv = sb("row_inv", [P, 2])
        with ExitStack() as early:
            w_q, w_k, w_v, w_pt = [early.enter_context(nc.sbuf_tensor(n, [P, KC, C], F32))
                                   for n in ("w_q", "w_k", "w_v", "w_pt")]
            x_0 = early.enter_context(nc.sbuf_tensor("x_0", [P, KC, N], F32))
            bias_dot = early.enter_context(nc.sbuf_tensor("bias_dot", [P, 3, C], F32))
        v_hi = sb("v_hi", [P, NT, C], F32R)
        v_lo = sb("v_lo", [P, NT, C], F32R)
        pt_hi = sb("pt_hi", [P, NT, HN], F32R)
        pt_lo = sb("pt_lo", [P, NT, HN], F32R)

        ps_e = ctx.enter_context(nc.psum_tensor("ps_e", [P, 2, N], F32))
        ps_a = ctx.enter_context(nc.psum_tensor("ps_a", [P, BANKS, HN], F32))

        s_vec = sem("s_vec")
        s_wq, s_wk, s_wv, s_wpt = sem("s_wq"), sem("s_wk"), sem("s_wv"), sem("s_wpt")
        s_x0 = [sem(f"s_x0{k}") for k in range(KC)]
        s_x = [sem(f"s_x{j}") for j in range(2)]
        s_res = [sem(f"s_res{g}") for g in range(2)]
        s_out = [sem(f"s_out{g}") for g in range(2)]
        s_spill = sem("s_spill")
        s_fetch = sem("s_fetch")
        s_const = sem("s_const")
        s_var_eps = sem("s_var_eps")
        s_rstd = sem("s_rstd")
        s_acc = sem("s_acc")
        s_e = sem("s_e")
        s_col = sem("s_col")
        s_whi = sem("s_whi")
        s_xhi = sem("s_xhi")
        s_uhi = sem("s_uhi")
        s_vhi = sem("s_vhi")
        s_exp = sem("s_exp")
        s_pthi = sem("s_pthi")
        s_free = sem("s_free")
        s_bias = sem("s_bias")
        s_bn = sem("s_bn")
        s_mv = sem("s_mv")
        s_mom1_hi = sem("s_mom1_hi")
        s_mom1 = sem("s_mom1")
        s_dev = sem("s_dev")
        s_sq = sem("s_sq")
        s_ex = sem("s_ex")
        s_mom2_hi = sem("s_mom2_hi")
        s_mom2 = sem("s_mom2")
        s_gain = sem("s_gain")
        s_y = sem("s_y")
        s_xlo = sem("s_xlo")
        s_kdot = sem("s_kdot")
        s_bdot = sem("s_bdot")
        s_colq = sem("s_colq")
        s_colhi = sem("s_colhi")
        s_collo = sem("s_collo")
        s_colout = sem("s_colout")
        s_max = sem("s_max")
        s_shift = sem("s_shift")
        s_inv = sem("s_inv")
        s_p = sem("s_p")
        s_blocks = sem("s_blocks")
        s_ptlo = sem("s_ptlo")

        block = ctx.enter_context(nc.Block())

        def image_rows(ap, b, chunk, n0, n):
            return ap[bass.ds(b, 1), chunk * P:(chunk + 1) * P, n0:n0 + n].rearrange("a p i -> p (a i)")

        @block.sync
        def _(sp):
            def load_pair(b, pair):
                for j in range(2):
                    if not (isinstance(b, int) and b == 1 and pair == 0):
                        sp.wait_ge(s_kdot, KC * b + 2 * pair + j - 1)
                    sp.dma_start(x_in[:, j, :], image_rows(x, b, 2 * pair + j, 0, N)).then_inc(s_x[j], 16)

            def load_residual(b, h, g):
                n = 2 * b + h
                if not (isinstance(b, int) and b == 0 and h == 0 and g < 2):
                    sp.wait_ge(s_out[g % 2], 16 * (2 * n + g // 2))
                sp.dma_start(res[:, g % 2, :], image_rows(x, b, g, h * HN, HN)).then_inc(s_res[g % 2], 16)

            def store(b, h, g, at):
                sp.wait_ge(s_free, at("O", h, g)[0] + 1)
                sp.dma_start(image_rows(out, b, g, h * HN, HN), res[:, g % 2, :]).then_inc(s_out[g % 2], 16)

            def spill(b, t):
                sp.wait_ge(s_blocks, NT * b + t + 1)
                for q in range(NQ):
                    sp.dma_start(scratch[t, :, :, q, :].rearrange("r b e -> b r e"),
                                 blocks_out[q * Q:(q + 1) * Q, :, :, :].rearrange("b r t a -> b r (t a)")
                                 ).then_inc(s_spill, 16)

            def fetch(b, t):
                sp.wait_ge(s_spill, 16 * NQ * (NT * b + t + 1))
                if t % 2:
                    sp.wait_ge(s_ptlo, NT * b + t)
                sp.dma_start(blocks_in[:].rearrange("p q t a -> p (q t a)"),
                             scratch[t].rearrange("r b q e -> (r b) (q e)")).then_inc(s_fetch, 16)

            def half(b, h, at, tiles, load):
                for n, (bt, t) in enumerate(tiles):
                    spill(bt, t)
                    if n < 3:
                        fetch(bt, t)
                for g in range(KC):
                    store(b, h, g, at)
                    if g < 2:
                        load_residual(b, h, g + 2)
                if len(tiles) == 4:
                    fetch(*tiles[3])
                if load:
                    load_pair(*load)

            def body(b, has_next, has_next2):
                at = turns(b, has_next, has_next2)
                half(b, 0, at, [(b, 2), (b, 3), (b, 4), (b, 5)], (b + 2, 0) if has_next2 else None)
                for g in range(2):
                    load_residual(b, 1, g)
                half(b, 1, at, [(b, 6), (b, 7)] + [(b + 1, 0), (b + 1, 1)] * has_next, (b + 2, 1) if has_next2 else None)
                if has_next:
                    for g in range(2):
                        load_residual(b + 1, 0, g)

            sp.dma_start(vec[:], vecs).then_inc(s_vec, 16)
            sp.dma_start(w_q[:], wq.rearrange("(k p) c -> p k c", p=P)).then_inc(s_wq, 16)
            for k in range(KC):
                sp.dma_start(x_0[:, k, :], image_rows(x, 0, k, 0, N)).then_inc(s_x0[k], 16)
            load_pair(1, 0)
            for g in range(2):
                load_residual(0, 0, g)
            load_pair(1, 1)
            for t in range(2):
                spill(0, t)
                fetch(0, t)
            with nc.sync.Fori(0, B // 2 - 1) as i:
                for p in range(2):
                    body(2 * i + p, True, True)
            body(B - 2, True, False)
            body(B - 1, False, False)
            for g in range(2):
                sp.wait_ge(s_out[g], 16 * 4 * B)

        @block.gpsimd
        def _(pool):
            done = [0]

            def step(instruction):
                instruction.then_inc(s_const, 1)
                done[0] += 1
                return done[0]

            step(nc.gpsimd.memset(eps[:], EPS))
            step(nc.gpsimd.memset(half_neg[:], -0.5))
            step(nc.gpsimd.memset(kdot[:, 0:P], 1.0 / GROUP))
            made = step(nc.gpsimd.memset(kdot[:, P:2 * P], 0.0))
            pool.wait_ge(s_const, made)
            blocks = kdot[:, 0:P].rearrange("p (g c) -> p g c", c=GROUP)
            made = step(nc.gpsimd.affine_select(out=blocks, in_=blocks, compare_op=ALU.is_ge, fill=0.0, base=0,
                                                pattern=[[-GROUP, P // GROUP], [0, GROUP]], channel_multiplier=1))
            pool.wait_ge(s_const, made)
            made = step(nc.gpsimd.affine_select(out=blocks, in_=blocks, compare_op=ALU.is_ge, fill=0.0, base=GROUP - 1,
                                                pattern=[[GROUP, P // GROUP], [0, GROUP]], channel_multiplier=-1))
            pool.wait_ge(s_const, made)
            step(nc.gpsimd.tensor_copy(avg[:], kdot[:, 0:P]))
            diagonals = kdot[:, P:2 * P]
            for m in range(1 - NQ, NQ):
                made = step(nc.gpsimd.affine_select(out=diagonals, in_=diagonals, compare_op=ALU.not_equal, fill=1.0,
                                                    base=Q * m, pattern=[[-1, P]], channel_multiplier=1))
                pool.wait_ge(s_const, made)
            made = step(nc.gpsimd.tensor_copy(same[:], diagonals))
            assert made == CONST_STEPS

            def root(s, n, at):
                pool.wait_ge(s_free, at + 1)
                nc.gpsimd.tensor_tensor(var_eps[:, 0:n], var[:, 0:n], eps[:, 0:n], ALU.add).then_inc(s_var_eps, 1)
                pool.wait_ge(s_var_eps, s + 1)
                nc.gpsimd.tensor_tensor(rstd[:, 0:n], var_eps[:, 0:n], half_neg[:, 0:n], ALU.pow).then_inc(s_rstd, 1)

            root(0, KC, FIRST[("S2", 0)])
            root(1, 2, FIRST[("S2", 1)])
            with nc.gpsimd.Fori(0, B // 2 - 1) as i:
                for p in range(2):
                    b = 2 * i + p
                    root(set_of(b + 1, 1), 2, turns(b)("S2", 0)[0])
                    root(set_of(b + 2, 0), 2, turns(b)("S2", 1)[0])
            root(set_of(B - 1, 1), 2, turns(B - 2, True, False)("S2", 0)[0])

        @block.tensor
        def _(pe):
            def product(acc, left_hi, left_lo, right_hi, right_lo, n, inc):
                for k in range(n):
                    nc.tensor.matmul(acc, left_hi(k), right_hi(k), start=(k == 0), stop=False)
                    nc.tensor.matmul(acc, left_hi(k), right_lo(k), start=False, stop=False)
                    last = nc.tensor.matmul(acc, left_lo(k), right_hi(k), start=False, stop=(k == n - 1))
                last.then_inc(inc, 1)

            def bank(index):
                return ps_a[:, index, :]

            def u_turn(b, p, h, g, at, index):
                pe.wait_ge(s_xlo, KC * b + KC)
                pe.wait_ge(s_free, at - BANKS + 1)
                cols = slice(g * P, (g + 1) * P)
                pix = slice(h * HN, (h + 1) * HN)
                product(bank(index), lambda k: g_hi[:, k, cols], lambda k: g_lo[:, k, cols],
                        lambda k: xn_hi[p][:, k, pix], lambda k: xn_lo[p][:, k, pix], KC, s_acc)

            def v_turn(p, j, at, index):
                pe.wait_ge(s_free, at - BANKS + 1)
                pix = slice(j * P, (j + 1) * P)
                product(bank(index), lambda k: xn_hi[p][:, k, pix], lambda k: xn_lo[p][:, k, pix],
                        lambda k: m_hi[:, k, :], lambda k: m_lo[:, k, :], KC, s_acc)

            def o_turn(b, h, g, at, index):
                pe.wait_ge(s_ptlo, NT * b + TH * h + TH)
                pe.wait_ge(s_free, at - BANKS + 1)
                cols = slice(g * P, (g + 1) * P)
                product(bank(index), lambda j: v_hi[:, j, cols], lambda j: v_lo[:, j, cols],
                        lambda j: pt_hi[:, j, :], lambda j: pt_lo[:, j, :], NT, s_acc)

            def column_sums(n, width):
                pe.wait_ge(s_collo, n + 1)
                out_ps = ps_e[:, 0, 0:width]
                nc.tensor.matmul(out_ps, same[:], col_hi[:, 0:width], start=True, stop=False)
                nc.tensor.matmul(out_ps, same[:], col_lo[:, 0:width], start=False, stop=True).then_inc(s_col, 1)

            def average(waited, s, n, at, index):
                pe.wait_ge(waited, s + 1)
                if not isinstance(at, int) or at >= BANKS:
                    pe.wait_ge(s_free, at - BANKS + 1)
                nc.tensor.matmul(bank(index)[:, 0:2 * n], avg[:], mom[:, 0:2 * n], start=True, stop=True).then_inc(s_acc, 1)

            def scores(b, p, t, u_turns=None):
                if t == 0:
                    pe.wait_ge(s_colout, b + 3)
                if not (isinstance(b, int) and b == 0 and t < 2):
                    pe.wait_ge(s_exp, NT * b + t - 1)
                tile = slice(t % TH * P, (t % TH + 1) * P)
                for k in range(KC):
                    if u_turns:
                        pe.wait_ge(s_free, u_turns[k] + 1)
                    for left, right, start, stop in ((u_hi, xn_hi[p], k == 0, False), (u_hi, xn_lo[p], False, False),
                                                     (u_lo, xn_hi[p], False, k == KC - 1)):
                        for jh in range(2):
                            pix = slice(jh * HN, (jh + 1) * HN)
                            last = nc.tensor.matmul(ps_e[:, t % 2, pix], left[:, k, tile], right[:, k, pix],
                                                    start=start, stop=stop)
                last.then_inc(s_e, 1)

            def body(b, p, has_next, has_next2):
                at = turns(b, has_next, has_next2)
                scores(b, p, 2)
                scores(b, p, 3)
                for g in range(KC):
                    u_turn(b, p, 1, g, *at("U", 1, g))
                    if has_next and g == 1:
                        average(s_mom1, set_of(b + 1, 1), 2, *at("S1", 0))
                scores(b, p, 4, [at("U", 1, g)[0] for g in range(KC)])
                if has_next:
                    average(s_mom2, set_of(b + 1, 1), 2, *at("S2", 0))
                scores(b, p, 5)
                for g in range(KC):
                    o_turn(b, 0, g, *at("O", 0, g))
                scores(b, p, 6)
                scores(b, p, 7)
                if has_next:
                    for g in range(KC):
                        u_turn(b + 1, 1 - p, 0, g, *at("U", 0, g))
                        if has_next2 and g == 1:
                            average(s_mom1, set_of(b + 2, 0), 2, *at("S1", 1))
                        if g == 2:
                            pe.wait_ge(s_exp, NT * b + NT - 1)
                            column_sums(b + 3, N // Q)
                    scores(b + 1, 1 - p, 0, [at("U", 0, g)[0] for g in range(KC)])
                    if has_next2:
                        average(s_mom2, set_of(b + 2, 0), 2, *at("S2", 1))
                    scores(b + 1, 1 - p, 1)
                for g in range(KC):
                    o_turn(b, 1, g, *at("O", 1, g))
                if has_next:
                    for j in range(NT):
                        v_turn(1 - p, j, *at("V", j))

            def weight_product(left, right, g, at, index):
                if at >= BANKS:
                    pe.wait_ge(s_free, at - BANKS + 1)
                for k in range(KC):
                    last = nc.tensor.matmul(bank(index), left[:, k, g * P:(g + 1) * P], right[:, k, :],
                                            start=(k == 0), stop=(k == KC - 1))
                last.then_inc(s_acc, 1)

            pe.wait_ge(s_const, CONST_STEPS)
            pe.wait_ge(s_wq, 16)
            pe.wait_ge(s_wk, 16)
            for g in range(KC):
                if g == 3:
                    average(s_mom1, 0, KC, *early_turn("S1", 0))
                weight_product(w_q, w_k, g, *early_turn("G", g))
            average(s_mom2, 0, KC, *early_turn("S2", 0))
            pe.wait_ge(s_wv, 16)
            pe.wait_ge(s_wpt, 16)
            for g in range(KC):
                weight_product(w_v, w_pt, g, *early_turn("M", g))
                if g == 1:
                    column_sums(0, 2 * C // Q)
            for g in range(KC):
                u_turn(0, 0, 0, g, *early_turn("U", g))
            pe.wait_ge(s_colout, 1)
            column_sums(1, C // Q)
            for j in range(NT):
                v_turn(0, j, *early_turn("V", j))
                if j == 2:
                    average(s_mom1, 1, 2, *early_turn("S1", 1))
                if j == 5:
                    average(s_mom2, 1, 2, *early_turn("S2", 1))
            pe.wait_ge(s_colout, 2)
            column_sums(2, N // Q)
            scores(0, 0, 0)
            scores(0, 0, 1)
            with nc.tensor.Fori(0, B // 2 - 1) as i:
                for p in range(2):
                    body(2 * i + p, p, True, True)
            body(B - 2, 0, True, False)
            body(B - 1, 1, False, False)

        @block.scalar
        def _(act):
            def split_x(b, p, chunk, src):
                act.wait_ge(s_y, KC * b + chunk + 1)
                nc.scalar.activation(xn_hi[p][:, chunk, :], src, ACT.Identity,
                                     bias=vec[:, BETA, chunk:chunk + 1]).then_inc(s_xhi, 1)

            def split_u(g, at, index):
                act.wait_ge(s_acc, at + 1)
                nc.scalar.activation(u_hi[:, g, :], ps_a[:, index, :], ACT.Identity,
                                     bias=u_bias[:, g:g + 1]).then_inc(s_uhi, 1)

            def split_v(j, at, index):
                act.wait_ge(s_acc, at + 1)
                nc.scalar.activation(v_hi[:, j, :], ps_a[:, index, :], ACT.Copy).then_inc(s_vhi, 1)

            def exponent(b, t):
                act.wait_ge(s_shift, NT * b + t + 1)
                nc.scalar.activation(prob[:], ps_e[:, t % 2, :], ACT.Exp, bias=neg_shift[:, t % 2:t % 2 + 1],
                                     accum_out=row_sum[:, t % 2:t % 2 + 1]).then_inc(s_exp, 1)

            def split_pt(b, t):
                act.wait_ge(s_fetch, 16 * (NT * b + t + 1))
                cols = slice(t % TH * P, (t % TH + 1) * P)
                nc.scalar.activation(pt_hi[:, :, cols].rearrange("p t (q a) -> p t q a", a=Q),
                                     blocks_in[:].rearrange("p q t a -> p t q a"), ACT.Copy).then_inc(s_pthi, 1)

            def half(b, h, at, tiles, next_split, u_turns, chunks):
                if next_split:
                    split_pt(*next_split)
                exponent(*tiles[0])
                exponent(*tiles[1])
                for g in range(KC):
                    if g == KC - 1:
                        split_pt(*tiles[0])
                    if u_turns:
                        split_u(g, *at("U", 1 - h, g))
                split_pt(*tiles[1])
                for tile in tiles[2:]:
                    exponent(*tile)
                for bx, px, chunk in chunks:
                    split_x(bx, px, chunk, x_in[:, chunk % 2, :])
                act.wait_ge(s_acc, at("O", h, KC - 1)[0] + 1)
                if len(tiles) == 4:
                    split_pt(*tiles[2])

            def body(b, p, has_next, has_next2):
                at = turns(b, has_next, has_next2)
                half(b, 0, at, [(b, 2), (b, 3), (b, 4), (b, 5)], None, True,
                     [(b + 1, 1 - p, c) for c in (2, 3)] if has_next else [])
                half(b, 1, at, [(b, 6), (b, 7)] + [(b + 1, 0), (b + 1, 1)] * has_next, (b, 5), has_next,
                     [(b + 2, p, c) for c in (0, 1)] if has_next2 else [])
                if has_next:
                    for j in range(NT):
                        split_v(j, *at("V", j))
                        if j == 1:
                            split_pt(b + 1, 1)

            act.dma_start(w_k[:], wk.rearrange("(k p) c -> p k c", p=P)).then_inc(s_wk, 16)
            act.dma_start(w_v[:], wv.rearrange("(k p) c -> p k c", p=P)).then_inc(s_wv, 16)
            act.dma_start(w_pt[:], wpt.rearrange("(k p) c -> p k c", p=P)).then_inc(s_wpt, 16)
            def split_weight(dst, g, scale, at, index):
                act.wait_ge(s_acc, at + 1)
                nc.scalar.activation(dst[:, g, :], ps_a[:, index, :], ACT.Copy, scale=scale).then_inc(s_whi, 1)

            for g in range(KC):
                split_weight(g_hi, g, SCALE, *early_turn("G", g))
            act.wait_ge(s_vec, 16)
            for g in range(KC):
                if g < 2:
                    split_x(0, 0, 2 * g, x_0[:, 2 * g, :])
                    split_x(0, 0, 2 * g + 1, x_0[:, 2 * g + 1, :])
                split_weight(m_hi, g, 1.0, *early_turn("M", g))
            act.wait_ge(s_bias, 2)
            for g in range(KC):
                split_u(g, *early_turn("U", g))
            for j in range(NT):
                split_v(j, *early_turn("V", j))
            for j in range(2):
                split_x(1, 1, j, x_in[:, j, :])
            exponent(0, 0)
            exponent(0, 1)
            split_pt(0, 0)
            split_pt(0, 1)
            with nc.scalar.Fori(0, B // 2 - 1) as i:
                for p in range(2):
                    body(2 * i + p, p, True, True)
            body(B - 2, 0, True, False)
            body(B - 1, 1, False, False)

        @block.vector
        def _(dve):
            def moments(src, k):
                for n in range(2):
                    last = nc.vector.bn_stats(bn[:, k, n * BN_OUT:(n + 1) * BN_OUT], src[:, n * HN:(n + 1) * HN])
                last.then_inc(s_bn, 1)

            def pair_moments(b, pair, j):
                dve.wait_ge(s_x[j], 16 * (set_of(b, pair)))
                moments(x_in[:, j, :], j)

            def aggregate(n):
                for k in range(n):
                    last = nc.vector.bn_aggr(mv[:, k, :], bn[:, k, :])
                last.then_inc(s_mv, 1)

            def split_moment(src, s, n, s_hi, s_lo):
                nc.vector.tensor_copy(mom[:, 0:n], src).then_inc(s_hi, 1)
                dve.wait_ge(s_hi, s + 1)
                nc.vector.tensor_tensor(mom[:, n:2 * n], src, mom[:, 0:n].bitcast(F32), ALU.subtract).then_inc(s_lo, 1)

            def split_mean(s, n):
                dve.wait_ge(s_mv, s + 1)
                split_moment(mv[:, 0:n, 0], s, n, s_mom1_hi, s_mom1)

            def gathered(dst, n, at, index):
                dve.wait_ge(s_acc, at + 1)
                nc.vector.tensor_reduce(dst[:, 0:n], ps_a[:, index, 0:2 * n].rearrange("p (s k) -> p k s", s=2),
                                        AX.X, ALU.add).then_inc(s_free, 1)

            def spread(s, n, at, index):
                gathered(mean, n, at, index)
                dve.wait_ge(s_free, at + 1)
                nc.vector.tensor_tensor(dev[:, 0:n], mv[:, 0:n, 0], mean[:, 0:n], ALU.subtract).then_inc(s_dev, 1)
                dve.wait_ge(s_dev, s + 1)
                nc.vector.tensor_tensor(sq[:, 0:n], dev[:, 0:n], dev[:, 0:n], ALU.mult).then_inc(s_sq, 1)
                dve.wait_ge(s_sq, s + 1)
                nc.vector.tensor_tensor(ex[:, 0:n], sq[:, 0:n], mv[:, 0:n, 1], ALU.add).then_inc(s_ex, 1)
                dve.wait_ge(s_ex, s + 1)
                split_moment(ex[:, 0:n], s, n, s_mom2_hi, s_mom2)

            def centre(s, n, k0, src):
                dve.wait_ge(s_rstd, s + 1)
                nc.vector.tensor_tensor(gain[:, 0:n], rstd[:, 0:n], vec[:, GAMMA, k0:k0 + n], ALU.mult).then_inc(s_gain, 1)
                dve.wait_ge(s_gain, s + 1)
                for k in range(n):
                    nc.vector.tensor_scalar(src[:, k, :], src[:, k, :], mean[:, k:k + 1], gain[:, k:k + 1],
                                            ALU.subtract, ALU.mult).then_inc(s_y, 1)

            def split_x(b, p, chunk, src):
                dve.wait_ge(s_xhi, KC * b + chunk + 1)
                nc.vector.scalar_tensor_tensor(out=xn_lo[p][:, chunk, :], in0=src,
                                               scalar=vec[:, BETA, chunk:chunk + 1],
                                               in1=xn_hi[p][:, chunk, :].bitcast(F32), op0=ALU.add,
                                               op1=ALU.subtract).then_inc(s_xlo, 1)

            def add_kdot(b, chunk, src):
                if chunk == 0:
                    nc.vector.tensor_scalar(kdot[:], src, k_row[:, 0:1], k_const[:],
                                            ALU.mult, ALU.add).then_inc(s_kdot, 1)
                else:
                    dve.wait_ge(s_kdot, KC * b + chunk)
                    nc.vector.scalar_tensor_tensor(out=kdot[:], in0=src,
                                                   scalar=k_row[:, chunk:chunk + 1], in1=kdot[:], op0=ALU.mult,
                                                   op1=ALU.add).then_inc(s_kdot, 1)

            def partial_sums(n, src, width):
                nc.vector.tensor_reduce(kdot_q[:, 0:width], src.rearrange("p (c r) -> p c r", r=Q), AX.X, ALU.add,
                                        apply_transpose=True).then_inc(s_colq, 1)
                dve.wait_ge(s_colq, n + 1)
                nc.vector.tensor_copy(col_hi[:, 0:width], kdot_q[:, 0:width]).then_inc(s_colhi, 1)
                dve.wait_ge(s_colhi, n + 1)
                nc.vector.tensor_tensor(col_lo[:, 0:width], kdot_q[:, 0:width], col_hi[:, 0:width].bitcast(F32),
                                        ALU.subtract).then_inc(s_collo, 1)

            def image_sums(b):
                dve.wait_ge(s_kdot, KC * b + KC)
                partial_sums(b + 2, kdot[:], N // Q)

            def read_columns(n, dst, width):
                dve.wait_ge(s_col, n + 1)
                for q in range(NQ):
                    rows = slice(q * Q, (q + 1) * Q)
                    last = nc.vector.tensor_copy(dst[rows, :], ps_e[rows, 0, 0:NQ * width].rearrange(
                        "p (j q) -> p j q", q=NQ)[:, :, q])
                last.then_inc(s_colout, 1)

            def split_u(b, h, g, index):
                dve.wait_ge(s_uhi, 2 * KC * b + KC * h + g + 1)
                nc.vector.scalar_tensor_tensor(out=u_lo[:, g, :], in0=ps_a[:, index, :], scalar=u_bias[:, g:g + 1],
                                               in1=u_hi[:, g, :].bitcast(F32), op0=ALU.add,
                                               op1=ALU.subtract).then_inc(s_free, 1)

            def split_v(b, j, index):
                dve.wait_ge(s_vhi, NT * b + j + 1)
                nc.vector.tensor_tensor(v_lo[:, j, :], ps_a[:, index, :], v_hi[:, j, :].bitcast(F32),
                                        ALU.subtract).then_inc(s_free, 1)

            def shift(b, p, t):
                dve.wait_ge(s_e, NT * b + t + 1)
                nc.vector.tensor_reduce(row_max[:, t % 2:t % 2 + 1], ps_e[:, t % 2, :], AX.X, ALU.max).then_inc(s_max, 1)
                dve.wait_ge(s_max, NT * b + t + 1)
                nc.vector.scalar_tensor_tensor(out=neg_shift[:, t % 2:t % 2 + 1], in0=row_max[:, t % 2:t % 2 + 1],
                                               scalar=t_bias[:, p, t:t + 1], in1=t_bias[:, p, t:t + 1], op0=ALU.add,
                                               op1=ALU.subtract, reverse1=True).then_inc(s_shift, 1)

            def normalise(b, t):
                dve.wait_ge(s_exp, NT * b + t + 1)
                nc.vector.reciprocal(row_inv[:, t % 2:t % 2 + 1], row_sum[:, t % 2:t % 2 + 1]).then_inc(s_inv, 1)
                dve.wait_ge(s_inv, NT * b + t + 1)
                nc.vector.tensor_scalar(prob[:], prob[:], row_inv[:, t % 2:t % 2 + 1], None, ALU.mult).then_inc(s_p, 1)

            def transpose_blocks(b, t):
                if not (isinstance(b, int) and b == 0 and t == 0):
                    dve.wait_ge(s_spill, 16 * NQ * (NT * b + t))
                dve.wait_ge(s_p, NT * b + t + 1)
                nc.vector.transpose(blocks_out[:].rearrange("p q t a -> p t q a"),
                                    prob[:].rearrange("p (t q a) -> p t q a", q=NQ, a=Q)).then_inc(s_blocks, 1)

            def split_pt(b, t):
                dve.wait_ge(s_pthi, NT * b + t + 1)
                cols = slice(t % TH * P, (t % TH + 1) * P)
                nc.vector.tensor_tensor(pt_lo[:, :, cols].rearrange("p t (q a) -> p t q a", a=Q),
                                        blocks_in[:].rearrange("p q t a -> p t q a"),
                                        pt_hi[:, :, cols].rearrange("p t (q a) -> p t q a", a=Q).bitcast(F32),
                                        ALU.subtract).then_inc(s_ptlo, 1)

            def result(b, h, g, at, index):
                dve.wait_ge(s_acc, at + 1)
                dve.wait_ge(s_res[g % 2], 16 * (4 * b + 2 * h + g // 2 + 1))
                nc.vector.scalar_tensor_tensor(out=res[:, g % 2, :], in0=ps_a[:, index, :], scalar=o_bias[:, g:g + 1],
                                               in1=res[:, g % 2, :], op0=ALU.add, op1=ALU.add).then_inc(s_free, 1)

            def half(b, p, h, at, tiles, next_split, stats, u_of):
                s = set_of(*stats) if stats else None

                def softmax(n, split=None, moment=None):
                    bt, pt, t = tiles[n]
                    shift(bt, pt, t)
                    if split:
                        split_pt(*split)
                    if moment is not None:
                        pair_moments(*stats, moment)
                        if moment == 1:
                            dve.wait_ge(s_bn, 2 * s + 4)
                    normalise(bt, t)
                    return bt, t

                transpose_blocks(*softmax(0, split=next_split, moment=0 if stats else None))
                last = softmax(1, moment=1 if stats else None)
                if stats:
                    aggregate(2)
                    split_mean(s, 2)
                if u_of:
                    split_u(*u_of, 0, at("U", 1 - h, 0)[1])
                transpose_blocks(*last)
                if u_of:
                    split_u(*u_of, 1, at("U", 1 - h, 1)[1])
                if stats:
                    spread(s, 2, *at("S1", h))
                if u_of:
                    split_u(*u_of, 2, at("U", 1 - h, 2)[1])
                    if h == 1:
                        read_columns(b + 3, t_bias[:, 1 - p, :], NT)
                split_pt(tiles[0][0], tiles[0][2])
                if u_of:
                    split_u(*u_of, 3, at("U", 1 - h, 3)[1])
                if len(tiles) == 4:
                    transpose_blocks(*softmax(2, split=(tiles[1][0], tiles[1][2])))
                    if stats:
                        gathered(var, 2, *at("S2", h))
                    transpose_blocks(*softmax(3))
                else:
                    split_pt(tiles[1][0], tiles[1][2])
                if stats:
                    bs, pair = stats
                    ps = (1 - p) if h == 0 else p
                    centre(s, 2, 2 * pair, x_in)
                    split_x(bs, ps, 2 * pair, x_in[:, 0, :])
                for g in range(KC):
                    result(b, h, g, *at("O", h, g))
                    if stats and g == 0:
                        add_kdot(bs, 2 * pair, x_in[:, 0, :])
                        split_x(bs, ps, 2 * pair + 1, x_in[:, 1, :])
                    if stats and g == 1:
                        add_kdot(bs, 2 * pair + 1, x_in[:, 1, :])
                    if stats and g == 2 and pair == 1:
                        image_sums(bs)
                if len(tiles) == 4:
                    split_pt(tiles[2][0], tiles[2][2])

            def body(b, p, has_next, has_next2):
                at = turns(b, has_next, has_next2)
                half(b, p, 0, at, [(b, p, t) for t in (2, 3, 4, 5)], None, (b + 1, 1) if has_next else None, (b, 1))
                half(b, p, 1, at, [(b, p, 6), (b, p, 7)] + [(b + 1, 1 - p, 0), (b + 1, 1 - p, 1)] * has_next, (b, 5),
                     (b + 2, 0) if has_next2 else None, (b + 1, 0) if has_next else None)
                if has_next:
                    for j in range(NT):
                        split_v(b + 1, j, at("V", j)[1])
                        if j == 1:
                            split_pt(b + 1, 1)

            def split_weight(dst_hi, dst_lo, g, scale, n, at, index):
                dve.wait_ge(s_whi, n + 1)
                nc.vector.scalar_tensor_tensor(out=dst_lo[:, g, :], in0=ps_a[:, index, :], scalar=scale,
                                               in1=dst_hi[:, g, :].bitcast(F32), op0=ALU.mult,
                                               op1=ALU.subtract).then_inc(s_free, 1)

            def bias_product(which, weight, column):
                for k in range(KC):
                    if k == 0:
                        nc.vector.tensor_scalar(bias_dot[:, which, :], weight[:, 0, :], vec[:, column, 0:1], None,
                                                ALU.mult).then_inc(s_bdot, 1)
                    else:
                        dve.wait_ge(s_bdot, KC * which + k)
                        nc.vector.scalar_tensor_tensor(out=bias_dot[:, which, :], in0=weight[:, k, :],
                                                       scalar=vec[:, column, k:k + 1], in1=bias_dot[:, which, :],
                                                       op0=ALU.mult, op1=ALU.add).then_inc(s_bdot, 1)

            dve.wait_ge(s_vec, 16)
            dve.wait_ge(s_wk, 16)
            bias_product(0, w_k, BQ)
            for k in range(KC):
                dve.wait_ge(s_x0[k], 16)
                moments(x_0[:, k, :], k)
                if k == 1:
                    split_weight(g_hi, g_lo, 0, SCALE, 0, *early_turn("G", 0))
            dve.wait_ge(s_bn, KC)
            aggregate(KC)
            split_mean(0, KC)
            split_weight(g_hi, g_lo, 1, SCALE, 1, *early_turn("G", 1))
            dve.wait_ge(s_wq, 16)
            bias_product(1, w_q, BK)
            dve.wait_ge(s_bdot, 2 * KC)
            partial_sums(0, bias_dot[:, 0:2, :].rearrange("p w c -> p (w c)"), 2 * C // Q)
            split_weight(g_hi, g_lo, 2, SCALE, 2, *early_turn("G", 2))
            spread(0, KC, *early_turn("S1", 0))
            split_weight(g_hi, g_lo, 3, SCALE, 3, *early_turn("G", 3))
            gathered(var, KC, *early_turn("S2", 0))
            centre(0, KC, 0, x_0)
            split_x(0, 0, 0, x_0[:, 0, :])
            split_x(0, 0, 1, x_0[:, 1, :])
            split_weight(m_hi, m_lo, 0, 1.0, KC, *early_turn("M", 0))
            split_x(0, 0, 2, x_0[:, 2, :])
            split_x(0, 0, 3, x_0[:, 3, :])
            split_weight(m_hi, m_lo, 1, 1.0, KC + 1, *early_turn("M", 1))
            read_columns(0, columns[:].rearrange("p w k -> p (w k)"), 2 * KC)
            dve.wait_ge(s_colout, 1)
            nc.vector.tensor_scalar(k_row[:], columns[:, 1, :], SCALE, None, ALU.mult).then_inc(s_bias, 1)
            nc.vector.tensor_scalar(u_bias[:], columns[:, 0, :], SCALE, None, ALU.mult).then_inc(s_bias, 1)
            nc.vector.tensor_tensor(k_tmp[:, 0, :], vec[:, BQ, :], vec[:, BK, :], ALU.mult).then_inc(s_bias, 1)
            dve.wait_ge(s_bias, 1)
            nc.vector.tensor_tensor(k_tmp[:, 1, :], k_row[:], vec[:, BETA, :], ALU.mult).then_inc(s_bias, 1)
            dve.wait_ge(s_bias, 4)
            nc.vector.tensor_reduce(k_sum[:], k_tmp[:], AX.X, ALU.add).then_inc(s_bias, 1)
            dve.wait_ge(s_bias, 5)
            nc.vector.scalar_tensor_tensor(out=k_const[:], in0=k_sum[:, 0:1], scalar=SCALE, in1=k_sum[:, 1:2],
                                           op0=ALU.mult, op1=ALU.add).then_inc(s_bias, 1)
            split_weight(m_hi, m_lo, 2, 1.0, KC + 2, *early_turn("M", 2))
            split_weight(m_hi, m_lo, 3, 1.0, KC + 3, *early_turn("M", 3))
            dve.wait_ge(s_wpt, 16)
            bias_product(2, w_pt, BV)
            split_u(0, 0, 0, early_turn("U", 0)[1])
            split_u(0, 0, 1, early_turn("U", 1)[1])
            dve.wait_ge(s_bdot, 3 * KC)
            partial_sums(1, bias_dot[:, 2, :], C // Q)
            split_u(0, 0, 2, early_turn("U", 2)[1])
            split_u(0, 0, 3, early_turn("U", 3)[1])
            for j in range(2):
                pair_moments(1, 0, j)
            dve.wait_ge(s_bn, KC + 2)
            aggregate(2)
            split_mean(1, 2)
            read_columns(1, columns[:, 0, :], KC)
            dve.wait_ge(s_colout, 2)
            nc.vector.tensor_tensor(o_bias[:], columns[:, 0, :], vec[:, BP, :], ALU.add).then_inc(s_bias, 1)
            dve.wait_ge(s_bias, 6)
            for j in range(NT):
                split_v(0, j, early_turn("V", j)[1])
                if j < KC:
                    add_kdot(0, j, x_0[:, j, :])
                if j == 2:
                    spread(1, 2, *early_turn("S1", 1))
                if j == 4:
                    image_sums(0)
                if j == 5:
                    gathered(var, 2, *early_turn("S2", 1))
            centre(1, 2, 0, x_in)
            read_columns(2, t_bias[:, 0, :], NT)
            for j in range(2):
                split_x(1, 1, j, x_in[:, j, :])
                add_kdot(1, j, x_in[:, j, :])
            for t in range(2):
                shift(0, 0, t)
                normalise(0, t)
                transpose_blocks(0, t)
            for t in range(2):
                split_pt(0, t)
            with nc.vector.Fori(0, B // 2 - 1) as i:
                for p in range(2):
                    body(2 * i + p, p, True, True)
            body(B - 2, 0, True, False)
            body(B - 1, 1, False, False)


def kernel(**inputs):
    import concourse.bacc as bacc
    from concourse.bass_utils import run_bass_kernel_spmd

    x = np.ascontiguousarray(inputs["x"])
    b, c, h, w = x.shape
    names = ("gn_gamma", "gn_beta", "bq", "bk", "bv", "bp")
    columns = [np.asarray(inputs["L0_conv_" + n]).reshape(-1, 128).T for n in names]
    arrays = {
        "x": x.reshape(b, c, h * w),
        "wq": np.ascontiguousarray(inputs["L0_conv_wq"]),
        "wk": np.ascontiguousarray(inputs["L0_conv_wk"]),
        "wv": np.ascontiguousarray(inputs["L0_conv_wv"]),
        "wp_t": np.ascontiguousarray(np.asarray(inputs["L0_conv_wp"]).T),
        "vecs": np.ascontiguousarray(np.stack(columns, axis=1)),
    }
    nc = bacc.Bacc("TRN2", target_bir_lowering=False, num_devices=1)
    args = [nc.dram_tensor(n, a.shape, mybir.dt.from_np(a.dtype), kind="ExternalInput").ap() for n, a in arrays.items()]
    out = nc.dram_tensor("out", (b, c, h * w), F32, kind="ExternalOutput").ap()
    scratch = nc.dram_tensor("scratch", (h * w // 128, 4, 32, 4, h * w // 4), F32, kind="Internal").ap()
    build(nc, *args, scratch, out)
    result = run_bass_kernel_spmd(nc, [arrays], core_ids=[0])
    return result.results[0]["out"].reshape(b, c, h, w)
```

```python
from contextlib import ExitStack

import numpy as np
import concourse.bass as bass
from concourse import mybir

F32 = mybir.dt.float32
F32R = mybir.dt.float32r
ALU = mybir.AluOpType
ACT = mybir.ActivationFunctionType
AX = mybir.AxisListType

GAMMA, BETA, BQ, BK, BV, BP = range(6)


def build(nc, x, wq, wk, wv, wpt, vecs, scratch, out):
    B, C, N = x.shape
    P = 128
    KC = C // P
    NT = N // P
    HN = N // 2
    TH = NT // 2
    GROUP = C // 32
    EPS = 1e-6
    SCALE = float(C) ** -0.5
    BN_OUT = 6
    Q = 32
    NQ = P // Q
    CONST_STEPS = 16
    WARM_UP = 5
    BANKS = 4

    def image_turns(has_next2):
        return ([("U", 1, 0), ("U", 1, 1), ("U", 1, 2), ("S1", 0), ("U", 1, 3), ("S2", 0)]
                + [("O", 0, g) for g in range(KC)]
                + [("U", 0, 0), ("U", 0, 1), ("U", 0, 2)] + [("S1", 1)] * has_next2 + [("U", 0, 3)]
                + [("S2", 1)] * has_next2 + [("O", 1, g) for g in range(KC)] + [("V", j) for j in range(NT)])

    LAST_TURNS = [("U", 1, g) for g in range(KC)] + [("O", h, g) for h in range(2) for g in range(KC)]
    TURNS = len(image_turns(True))
    FIRST = {what: n for n, what in enumerate(
        [("G", g) for g in range(KC)] + [("S1", 0), ("M", 0), ("S2", 0)] + [("M", g) for g in range(1, KC)]
        + [("U", g) for g in range(KC)] + [("V", 0), ("V", 1), ("V", 2), ("S1", 1), ("V", 3), ("V", 4), ("V", 5),
                                           ("S2", 1), ("V", 6), ("V", 7)])}
    assert TURNS % BANKS == 0 and len(FIRST) % BANKS == 0

    def turns(b, has_next2=True):
        start, shift, order = len(FIRST) + TURNS * b, 0, image_turns(has_next2)
        if isinstance(b, int) and b == B - 1:
            shift, order = len(image_turns(False)) - TURNS, LAST_TURNS
        table = {what: n for n, what in enumerate(order)}
        return lambda *what: (start + shift + table[what], (shift + table[what]) % BANKS)

    def early_turn(*what):
        return FIRST[what], FIRST[what] % BANKS

    def set_of(b, pair):
        return 2 * b + pair - 1

    ctx = ExitStack()
    with ctx:
        def sb(name, shape, dt=F32):
            return ctx.enter_context(nc.sbuf_tensor(name, shape, dt))

        def sem(name):
            return ctx.enter_context(nc.semaphore(name))

        x_in = sb("x_in", [P, 2, N])
        xn_hi = [sb(f"xn_hi{p}", [P, KC, N], F32R) for p in range(2)]
        xn_lo = [sb(f"xn_lo{p}", [P, KC, N], F32R) for p in range(2)]
        u_hi = sb("u_hi", [P, KC, HN], F32R)
        u_lo = sb("u_lo", [P, KC, HN], F32R)
        prob = sb("prob", [P, N])
        blocks_out = sb("blocks_out", [P, NQ, NT, Q])
        blocks_in = sb("blocks_in", [P, NQ, NT, Q])
        g_hi = sb("g_hi", [P, KC, C], F32R)
        g_lo = sb("g_lo", [P, KC, C], F32R)
        m_hi = sb("m_hi", [P, KC, C], F32R)
        m_lo = sb("m_lo", [P, KC, C], F32R)
        res = sb("res", [P, 2, HN])
        kdot = sb("kdot", [P, N])
        kdot_q = sb("kdot_q", [P, 3 * C // Q])
        col_hi = sb("col_hi", [P, 3 * C // Q], F32R)
        col_lo = sb("col_lo", [P, 3 * C // Q], F32R)
        avg = sb("avg", [P, P], F32R)
        same = sb("same", [P, P], F32R)
        vec = sb("vec", [P, 6, KC])
        u_bias = sb("u_bias", [P, KC])
        k_row = sb("k_row", [P, KC])
        o_bias = sb("o_bias", [P, KC])
        k_tmp = sb("k_tmp", [P, 2, KC])
        k_sum = sb("k_sum", [P, 2])
        k_const = sb("k_const", [P, 1])
        columns = sb("columns", [P, 3, KC])
        t_bias = sb("t_bias", [P, 2, NT])
        bn = sb("bn", [P, KC, 2 * BN_OUT])
        mv = sb("mv", [P, KC, 2])
        mom = sb("mom", [P, 2 * KC], F32R)
        mean = sb("mean", [P, KC])
        dev = sb("dev", [P, KC])
        sq = sb("sq", [P, KC])
        ex = sb("ex", [P, KC])
        var = sb("var", [P, KC])
        var_eps = sb("var_eps", [P, KC])
        eps = sb("eps", [P, KC])
        half_neg = sb("half_neg", [P, KC])
        rstd = sb("rstd", [P, KC])
        gain = sb("gain", [P, KC])
        row_max = sb("row_max", [P, 2])
        neg_shift = sb("neg_shift", [P, 2])
        row_sum = sb("row_sum", [P, 2])
        row_inv = sb("row_inv", [P, 2])
        with ExitStack() as early:
            w_q, w_k, w_v, w_pt = [early.enter_context(nc.sbuf_tensor(n, [P, KC, C], F32))
                                   for n in ("w_q", "w_k", "w_v", "w_pt")]
            x_0 = early.enter_context(nc.sbuf_tensor("x_0", [P, KC, N], F32))
            bias_dot = early.enter_context(nc.sbuf_tensor("bias_dot", [P, 3, C], F32))
        v_hi = sb("v_hi", [P, NT, C], F32R)
        v_lo = sb("v_lo", [P, NT, C], F32R)
        pt_hi = sb("pt_hi", [P, NT, HN], F32R)
        pt_lo = sb("pt_lo", [P, NT, HN], F32R)
        spare = [buf[:].rearrange("p k (h n) -> p (k h) n", h=2) for buf in (xn_hi[B % 2], xn_lo[B % 2])]

        def pt_of(b, t):
            last = isinstance(b, int) and b == B - 1 and t >= TH
            return [half[:, :, t % TH * P:(t % TH + 1) * P] for half in (spare if last else (pt_hi, pt_lo))]

        ps_e = ctx.enter_context(nc.psum_tensor("ps_e", [P, 2, N], F32))
        ps_a = ctx.enter_context(nc.psum_tensor("ps_a", [P, BANKS, HN], F32))

        s_vec = sem("s_vec")
        s_wq = [sem(f"s_wq{k}") for k in range(KC)]
        s_wk = [sem(f"s_wk{k}") for k in range(KC)]
        s_wv, s_wpt = sem("s_wv"), sem("s_wpt")
        s_x0 = [sem(f"s_x0{k}") for k in range(KC)]
        s_x = [sem(f"s_x{j}") for j in range(2)]
        s_res = [sem(f"s_res{g}") for g in range(2)]
        s_out = [sem(f"s_out{g}") for g in range(2)]
        s_spill = sem("s_spill")
        s_fetch = sem("s_fetch")
        s_const = sem("s_const")
        s_var_eps = sem("s_var_eps")
        s_rstd = sem("s_rstd")
        s_acc = sem("s_acc")
        s_e = sem("s_e")
        s_col = sem("s_col")
        s_whi = sem("s_whi")
        s_xhi = sem("s_xhi")
        s_uhi = sem("s_uhi")
        s_vhi = sem("s_vhi")
        s_exp = sem("s_exp")
        s_pthi = sem("s_pthi")
        s_free = sem("s_free")
        s_bias = sem("s_bias")
        s_bn = sem("s_bn")
        s_mv = sem("s_mv")
        s_mom1_hi = sem("s_mom1_hi")
        s_mom1 = sem("s_mom1")
        s_dev = sem("s_dev")
        s_sq = sem("s_sq")
        s_ex = sem("s_ex")
        s_mom2_hi = sem("s_mom2_hi")
        s_mom2 = sem("s_mom2")
        s_gain = sem("s_gain")
        s_y = sem("s_y")
        s_xlo = sem("s_xlo")
        s_kdot = sem("s_kdot")
        s_bdot = sem("s_bdot")
        s_colq = sem("s_colq")
        s_colhi = sem("s_colhi")
        s_collo = sem("s_collo")
        s_colout = sem("s_colout")
        s_max = sem("s_max")
        s_shift = sem("s_shift")
        s_inv = sem("s_inv")
        s_p = sem("s_p")
        s_blocks = sem("s_blocks")
        s_ptlo = sem("s_ptlo")

        block = ctx.enter_context(nc.Block())

        def image_rows(ap, b, chunk, n0, n):
            return ap[bass.ds(b, 1), chunk * P:(chunk + 1) * P, n0:n0 + n].rearrange("a p i -> p (a i)")

        @block.sync
        def _(sp):
            def load_pair(b, pair):
                for j in range(2):
                    if not (isinstance(b, int) and b == 1 and pair == 0):
                        sp.wait_ge(s_kdot, KC * b + 2 * pair + j - 1)
                    sp.dma_start(x_in[:, j, :], image_rows(x, b, 2 * pair + j, 0, N)).then_inc(s_x[j], 16)

            def load_residual(b, h, g):
                n = 2 * b + h
                if not (isinstance(b, int) and b == 0 and h == 0 and g < 2):
                    sp.wait_ge(s_out[g % 2], 16 * (2 * n + g // 2))
                sp.dma_start(res[:, g % 2, :], image_rows(x, b, g, h * HN, HN)).then_inc(s_res[g % 2], 16)

            def store(b, h, g, at):
                sp.wait_ge(s_free, at("O", h, g)[0] + 1)
                sp.dma_start(image_rows(out, b, g, h * HN, HN), res[:, g % 2, :]).then_inc(s_out[g % 2], 16)

            def spill(b, t):
                sp.wait_ge(s_blocks, NT * b + t + 1)
                for q in range(NQ):
                    sp.dma_start(scratch[t, :, :, q, :].rearrange("r b e -> b r e"),
                                 blocks_out[q * Q:(q + 1) * Q, :, :, :].rearrange("b r t a -> b r (t a)")
                                 ).then_inc(s_spill, 16)

            def fetch(b, t):
                sp.wait_ge(s_spill, 16 * NQ * (NT * b + t + 1))
                if t % 2 or isinstance(b, int) and b == B - 1:
                    sp.wait_ge(s_ptlo, NT * b + t)
                sp.dma_start(blocks_in[:].rearrange("p q t a -> p (q t a)"),
                             scratch[t].rearrange("r b q e -> (r b) (q e)")).then_inc(s_fetch, 16)

            def half(b, h, at, tiles, load):
                for n, (bt, t) in enumerate(tiles):
                    spill(bt, t)
                    if n < 3:
                        fetch(bt, t)
                for g in range(KC):
                    store(b, h, g, at)
                    if g < 2:
                        load_residual(b, h, g + 2)
                fetch(*tiles[3])
                if load:
                    load_pair(*load)

            def body(b, has_next2):
                at = turns(b, has_next2)
                half(b, 0, at, [(b, 2), (b, 3), (b, 4), (b, 5)], (b + 2, 0) if has_next2 else None)
                for g in range(2):
                    load_residual(b, 1, g)
                half(b, 1, at, [(b, 6), (b, 7), (b + 1, 0), (b + 1, 1)], (b + 2, 1) if has_next2 else None)
                for g in range(2):
                    load_residual(b + 1, 0, g)

            def last_body(b):
                at = turns(b)
                for t in range(2, NT):
                    spill(b, t)
                    fetch(b, t)
                for h in range(2):
                    for g in range(KC):
                        store(b, h, g, at)
                        if (h, g) < (1, 2):
                            load_residual(b, (4 * h + g + 2) // 4, (g + 2) % 4)

            sp.dma_start(vec[:], vecs).then_inc(s_vec, 16)
            for k in range(KC):
                sp.dma_start(w_q[:, k, :], wq[k * P:(k + 1) * P, :]).then_inc(s_wq[k], 16)
            for k in range(0, KC, 2):
                sp.dma_start(x_0[:, k, :], image_rows(x, 0, k, 0, N)).then_inc(s_x0[k], 16)
            sp.dma_start(w_pt[:], wpt.rearrange("(k p) c -> p k c", p=P)).then_inc(s_wpt, 16)
            load_pair(1, 0)
            for g in range(2):
                load_residual(0, 0, g)
            for t in range(2):
                spill(0, t)
                fetch(0, t)
            load_pair(1, 1)
            with nc.sync.Fori(0, B // 2 - 1) as i:
                for p in range(2):
                    body(2 * i + p, True)
            body(B - 2, False)
            last_body(B - 1)
            for g in range(2):
                sp.wait_ge(s_out[g], 16 * 4 * B)

        @block.gpsimd
        def _(pool):
            done = [0]

            def step(instruction):
                instruction.then_inc(s_const, 1)
                done[0] += 1
                return done[0]

            step(nc.gpsimd.memset(kdot[:, 2 * P:], 0.0))
            step(nc.gpsimd.memset(eps[:], EPS))
            step(nc.gpsimd.memset(half_neg[:], -0.5))
            step(nc.gpsimd.memset(kdot[:, 0:P], 1.0 / GROUP))
            made = step(nc.gpsimd.memset(kdot[:, P:2 * P], 0.0))
            pool.wait_ge(s_const, made)
            blocks = kdot[:, 0:P].rearrange("p (g c) -> p g c", c=GROUP)
            made = step(nc.gpsimd.affine_select(out=blocks, in_=blocks, compare_op=ALU.is_ge, fill=0.0, base=0,
                                                pattern=[[-GROUP, P // GROUP], [0, GROUP]], channel_multiplier=1))
            pool.wait_ge(s_const, made)
            made = step(nc.gpsimd.affine_select(out=blocks, in_=blocks, compare_op=ALU.is_ge, fill=0.0, base=GROUP - 1,
                                                pattern=[[GROUP, P // GROUP], [0, GROUP]], channel_multiplier=-1))
            pool.wait_ge(s_const, made)
            step(nc.gpsimd.tensor_copy(avg[:], kdot[:, 0:P]))
            diagonals = kdot[:, P:2 * P]
            for m in range(1 - NQ, NQ):
                made = step(nc.gpsimd.affine_select(out=diagonals, in_=diagonals, compare_op=ALU.not_equal, fill=1.0,
                                                    base=Q * m, pattern=[[-1, P]], channel_multiplier=1))
                pool.wait_ge(s_const, made)
            made = step(nc.gpsimd.tensor_copy(same[:], diagonals))
            assert made == CONST_STEPS

            def root(s, n, at):
                pool.wait_ge(s_free, at + 1)
                nc.gpsimd.tensor_tensor(var_eps[:, 0:n], var[:, 0:n], eps[:, 0:n], ALU.add).then_inc(s_var_eps, 1)
                pool.wait_ge(s_var_eps, s + 1)
                nc.gpsimd.tensor_tensor(rstd[:, 0:n], var_eps[:, 0:n], half_neg[:, 0:n], ALU.pow).then_inc(s_rstd, 1)

            root(0, KC, FIRST[("S2", 0)])
            root(1, 2, FIRST[("S2", 1)])
            with nc.gpsimd.Fori(0, B // 2 - 1) as i:
                for p in range(2):
                    b = 2 * i + p
                    root(set_of(b + 1, 1), 2, turns(b)("S2", 0)[0])
                    root(set_of(b + 2, 0), 2, turns(b)("S2", 1)[0])
            root(set_of(B - 1, 1), 2, turns(B - 2, False)("S2", 0)[0])

        @block.tensor
        def _(pe):
            def product(acc, left_hi, left_lo, right_hi, right_lo, n, inc, image_0_chunks=False):
                for k in range(n):
                    if image_0_chunks:
                        pe.wait_ge(s_xlo, k + 1)
                    nc.tensor.matmul(acc, left_hi(k), right_hi(k), start=(k == 0), stop=False)
                    nc.tensor.matmul(acc, left_hi(k), right_lo(k), start=False, stop=False)
                    last = nc.tensor.matmul(acc, left_lo(k), right_hi(k), start=False, stop=(k == n - 1))
                last.then_inc(inc, 1)

            def bank(index):
                return ps_a[:, index, :]

            def u_turn(b, p, h, g, at, index):
                first = isinstance(b, int) and b == 0 and h == 0 and g == 0
                if not first:
                    pe.wait_ge(s_xlo, KC * b + KC)
                pe.wait_ge(s_free, at - BANKS + 1)
                cols = slice(g * P, (g + 1) * P)
                pix = slice(h * HN, (h + 1) * HN)
                product(bank(index), lambda k: g_hi[:, k, cols], lambda k: g_lo[:, k, cols],
                        lambda k: xn_hi[p][:, k, pix], lambda k: xn_lo[p][:, k, pix], KC, s_acc, image_0_chunks=first)

            def v_turn(p, j, at, index):
                pe.wait_ge(s_free, at - BANKS + 1)
                pix = slice(j * P, (j + 1) * P)
                product(bank(index), lambda k: xn_hi[p][:, k, pix], lambda k: xn_lo[p][:, k, pix],
                        lambda k: m_hi[:, k, :], lambda k: m_lo[:, k, :], KC, s_acc)

            def o_turn(b, h, g, at, index):
                pe.wait_ge(s_ptlo, NT * b + TH * h + TH)
                pe.wait_ge(s_free, at - BANKS + 1)
                cols = slice(g * P, (g + 1) * P)
                hi, lo = spare if isinstance(b, int) and b == B - 1 and h == 1 else (pt_hi, pt_lo)
                product(bank(index), lambda j: v_hi[:, j, cols], lambda j: v_lo[:, j, cols],
                        lambda j: hi[:, j, :], lambda j: lo[:, j, :], NT, s_acc)

            def column_sums(n, width, slot=0):
                pe.wait_ge(s_collo, n + 1)
                out_ps = ps_e[:, slot, 0:width]
                nc.tensor.matmul(out_ps, same[:], col_hi[:, 0:width], start=True, stop=False)
                nc.tensor.matmul(out_ps, same[:], col_lo[:, 0:width], start=False, stop=True).then_inc(s_col, 1)

            def average(waited, s, n, at, index):
                pe.wait_ge(waited, s + 1)
                pe.wait_ge(s_free, at - BANKS + 1)
                nc.tensor.matmul(bank(index)[:, 0:2 * n], avg[:], mom[:, 0:2 * n], start=True, stop=True).then_inc(s_acc, 1)

            def scores(b, p, t, u_turns=None):
                if t == 0 and not (isinstance(b, int) and b == 0):
                    pe.wait_ge(s_colout, b + 2)
                if not (isinstance(b, int) and b == 0 and t < 2):
                    pe.wait_ge(s_exp, NT * b + t - 1)
                tile = slice(t % TH * P, (t % TH + 1) * P)
                for k in range(KC):
                    if u_turns:
                        pe.wait_ge(s_free, u_turns[k] + 1)
                    for left, right, start, stop in ((u_hi, xn_hi[p], k == 0, False), (u_hi, xn_lo[p], False, False),
                                                     (u_lo, xn_hi[p], False, k == KC - 1)):
                        for jh in range(2):
                            pix = slice(jh * HN, (jh + 1) * HN)
                            last = nc.tensor.matmul(ps_e[:, t % 2, pix], left[:, k, tile], right[:, k, pix],
                                                    start=start, stop=stop)
                last.then_inc(s_e, 1)

            def body(b, p, has_next2):
                at = turns(b, has_next2)
                scores(b, p, 2)
                scores(b, p, 3)
                for g in range(KC):
                    u_turn(b, p, 1, g, *at("U", 1, g))
                    if g == 2:
                        average(s_mom1, set_of(b + 1, 1), 2, *at("S1", 0))
                scores(b, p, 4, [at("U", 1, g)[0] for g in range(KC)])
                average(s_mom2, set_of(b + 1, 1), 2, *at("S2", 0))
                scores(b, p, 5)
                for g in range(KC):
                    o_turn(b, 0, g, *at("O", 0, g))
                scores(b, p, 6)
                scores(b, p, 7)
                for g in range(KC):
                    u_turn(b + 1, 1 - p, 0, g, *at("U", 0, g))
                    if g == 2:
                        pe.wait_ge(s_exp, NT * b + NT - 1)
                        column_sums(b + 2, N // Q)
                        if has_next2:
                            average(s_mom1, set_of(b + 2, 0), 2, *at("S1", 1))
                scores(b + 1, 1 - p, 0, [at("U", 0, g)[0] for g in range(KC)])
                if has_next2:
                    average(s_mom2, set_of(b + 2, 0), 2, *at("S2", 1))
                scores(b + 1, 1 - p, 1)
                for g in range(KC):
                    o_turn(b, 1, g, *at("O", 1, g))
                for j in range(NT):
                    v_turn(1 - p, j, *at("V", j))

            def last_body(b, p):
                at = turns(b)
                scores(b, p, 2)
                scores(b, p, 3)
                for g in range(KC):
                    u_turn(b, p, 1, g, *at("U", 1, g))
                scores(b, p, 4, [at("U", 1, g)[0] for g in range(KC)])
                for t in range(5, NT):
                    scores(b, p, t)
                for h in range(2):
                    for g in range(KC):
                        o_turn(b, h, g, *at("O", h, g))

            pe.wait_ge(s_const, 1)
            for _ in range(WARM_UP):
                nc.tensor.matmul(ps_e[:, 1, 0:2 * P], kdot[:, 2 * P:3 * P], kdot[:, 2 * P:4 * P], start=True, stop=True)
            for k in range(KC):
                pe.wait_ge(s_wq[k], 16)
                pe.wait_ge(s_wk[k], 16)
                for g in range(KC):
                    last = nc.tensor.matmul(bank(early_turn("G", g)[1]), w_q[:, k, g * P:(g + 1) * P], w_k[:, k, :],
                                            start=(k == 0), stop=(k == KC - 1))
                    if k == KC - 1:
                        last.then_inc(s_acc, 1)
            pe.wait_ge(s_const, CONST_STEPS)
            average(s_mom1, 0, KC, *early_turn("S1", 0))
            pe.wait_ge(s_wv, 16)
            pe.wait_ge(s_wpt, 16)
            for g in range(KC):
                at, index = early_turn("M", g)
                pe.wait_ge(s_free, at - BANKS + 1)
                for k in range(KC):
                    last = nc.tensor.matmul(bank(index), w_v[:, k, g * P:(g + 1) * P], w_pt[:, k, :],
                                            start=(k == 0), stop=(k == KC - 1))
                last.then_inc(s_acc, 1)
                if g == 0:
                    average(s_mom2, 0, KC, *early_turn("S2", 0))
                if g == 2:
                    column_sums(0, 3 * C // Q)
            for g in range(KC):
                u_turn(0, 0, 0, g, *early_turn("U", g))
            pe.wait_ge(s_colout, 1)
            scores(0, 0, 0, [early_turn("U", g)[0] for g in range(KC)])
            column_sums(1, N // Q, slot=1)
            pe.wait_ge(s_colout, 2)
            scores(0, 0, 1)
            for j in range(NT):
                v_turn(0, j, *early_turn("V", j))
                if j == 2:
                    average(s_mom1, 1, 2, *early_turn("S1", 1))
                if j == 5:
                    average(s_mom2, 1, 2, *early_turn("S2", 1))
            with nc.tensor.Fori(0, B // 2 - 1) as i:
                for p in range(2):
                    body(2 * i + p, p, True)
            body(B - 2, 0, False)
            last_body(B - 1, 1)

        @block.scalar
        def _(act):
            def split_x(b, p, chunk, src):
                act.wait_ge(s_y, KC * b + chunk + 1)
                nc.scalar.activation(xn_hi[p][:, chunk, :], src, ACT.Identity,
                                     bias=vec[:, BETA, chunk:chunk + 1]).then_inc(s_xhi, 1)

            def split_u(g, at, index):
                act.wait_ge(s_acc, at + 1)
                nc.scalar.activation(u_hi[:, g, :], ps_a[:, index, :], ACT.Identity,
                                     bias=u_bias[:, g:g + 1]).then_inc(s_uhi, 1)

            def split_v(j, at, index):
                act.wait_ge(s_acc, at + 1)
                nc.scalar.activation(v_hi[:, j, :], ps_a[:, index, :], ACT.Copy).then_inc(s_vhi, 1)

            def exponent(b, t):
                act.wait_ge(s_shift, NT * b + t + 1)
                nc.scalar.activation(prob[:], ps_e[:, t % 2, :], ACT.Exp, bias=neg_shift[:, t % 2:t % 2 + 1],
                                     accum_out=row_sum[:, t % 2:t % 2 + 1]).then_inc(s_exp, 1)

            def split_pt(b, t):
                act.wait_ge(s_fetch, 16 * (NT * b + t + 1))
                nc.scalar.activation(pt_of(b, t)[0].rearrange("p t (q a) -> p t q a", a=Q),
                                     blocks_in[:].rearrange("p q t a -> p t q a"), ACT.Copy).then_inc(s_pthi, 1)

            def half(b, h, at, tiles, next_split, chunks):
                if next_split:
                    split_pt(*next_split)
                exponent(*tiles[0])
                exponent(*tiles[1])
                for g in range(KC):
                    split_u(g, *at("U", 1 - h, g))
                split_pt(*tiles[0])
                split_pt(*tiles[1])
                for tile in tiles[2:]:
                    exponent(*tile)
                for bx, px, chunk in chunks:
                    split_x(bx, px, chunk, x_in[:, chunk % 2, :])
                act.wait_ge(s_acc, at("O", h, KC - 1)[0] + 1)
                split_pt(*tiles[2])

            def body(b, p, has_next2):
                at = turns(b, has_next2)
                half(b, 0, at, [(b, 2), (b, 3), (b, 4), (b, 5)], None, [(b + 1, 1 - p, c) for c in (2, 3)])
                half(b, 1, at, [(b, 6), (b, 7), (b + 1, 0), (b + 1, 1)], (b, 5),
                     [(b + 2, p, c) for c in (0, 1)] if has_next2 else [])
                for j in range(NT):
                    split_v(j, *at("V", j))
                    if j == 1:
                        split_pt(b + 1, 1)

            def last_body(b):
                at = turns(b)
                exponent(b, 2)
                exponent(b, 3)
                for g in range(KC):
                    if g == KC - 1:
                        split_pt(b, 2)
                    split_u(g, *at("U", 1, g))
                split_pt(b, 3)
                for t in range(4, NT):
                    exponent(b, t)
                    if t >= 6:
                        split_pt(b, t - 2)
                split_pt(b, 6)
                split_pt(b, 7)

            for k in range(KC):
                act.dma_start(w_k[:, k, :], wk[k * P:(k + 1) * P, :]).then_inc(s_wk[k], 16)
            for k in range(1, KC, 2):
                act.dma_start(x_0[:, k, :], image_rows(x, 0, k, 0, N)).then_inc(s_x0[k], 16)
            act.dma_start(w_v[:], wv.rearrange("(k p) c -> p k c", p=P)).then_inc(s_wv, 16)
            def split_weight(dst, g, scale, at, index):
                act.wait_ge(s_acc, at + 1)
                nc.scalar.activation(dst[:, g, :], ps_a[:, index, :], ACT.Copy, scale=scale).then_inc(s_whi, 1)

            for g in range(KC):
                split_weight(g_hi, g, SCALE, *early_turn("G", g))
            act.wait_ge(s_vec, 16)
            for g in range(KC):
                split_weight(m_hi, g, 1.0, *early_turn("M", g))
                if g < 2:
                    split_x(0, 0, 2 * g, x_0[:, 2 * g, :])
                    split_x(0, 0, 2 * g + 1, x_0[:, 2 * g + 1, :])
            act.wait_ge(s_bias, 2)
            for g in range(KC):
                split_u(g, *early_turn("U", g))
            exponent(0, 0)
            exponent(0, 1)
            for j in range(NT):
                split_v(j, *early_turn("V", j))
                if j == 2:
                    split_pt(0, 0)
                if j == 6:
                    split_pt(0, 1)
            for j in range(2):
                split_x(1, 1, j, x_in[:, j, :])
            with nc.scalar.Fori(0, B // 2 - 1) as i:
                for p in range(2):
                    body(2 * i + p, p, True)
            body(B - 2, 0, False)
            last_body(B - 1)

        @block.vector
        def _(dve):
            def moments(src, k):
                for n in range(2):
                    last = nc.vector.bn_stats(bn[:, k, n * BN_OUT:(n + 1) * BN_OUT], src[:, n * HN:(n + 1) * HN])
                last.then_inc(s_bn, 1)

            def pair_moments(b, pair, j):
                dve.wait_ge(s_x[j], 16 * (set_of(b, pair)))
                moments(x_in[:, j, :], j)

            def aggregate(n):
                for k in range(n):
                    last = nc.vector.bn_aggr(mv[:, k, :], bn[:, k, :])
                last.then_inc(s_mv, 1)

            def split_moment(src, s, n, s_hi, s_lo):
                nc.vector.tensor_copy(mom[:, 0:n], src).then_inc(s_hi, 1)
                dve.wait_ge(s_hi, s + 1)
                nc.vector.tensor_tensor(mom[:, n:2 * n], src, mom[:, 0:n].bitcast(F32), ALU.subtract).then_inc(s_lo, 1)

            def split_mean(s, n):
                dve.wait_ge(s_mv, s + 1)
                split_moment(mv[:, 0:n, 0], s, n, s_mom1_hi, s_mom1)

            def gathered(dst, n, at, index):
                dve.wait_ge(s_acc, at + 1)
                nc.vector.tensor_reduce(dst[:, 0:n], ps_a[:, index, 0:2 * n].rearrange("p (s k) -> p k s", s=2),
                                        AX.X, ALU.add).then_inc(s_free, 1)

            def spread(s, n, at, index):
                gathered(mean, n, at, index)
                dve.wait_ge(s_free, at + 1)
                nc.vector.tensor_tensor(dev[:, 0:n], mv[:, 0:n, 0], mean[:, 0:n], ALU.subtract).then_inc(s_dev, 1)
                dve.wait_ge(s_dev, s + 1)
                nc.vector.tensor_tensor(sq[:, 0:n], dev[:, 0:n], dev[:, 0:n], ALU.mult).then_inc(s_sq, 1)
                dve.wait_ge(s_sq, s + 1)
                nc.vector.tensor_tensor(ex[:, 0:n], sq[:, 0:n], mv[:, 0:n, 1], ALU.add).then_inc(s_ex, 1)
                dve.wait_ge(s_ex, s + 1)
                split_moment(ex[:, 0:n], s, n, s_mom2_hi, s_mom2)

            def centre(s, n, k0, src):
                dve.wait_ge(s_rstd, s + 1)
                nc.vector.tensor_tensor(gain[:, 0:n], rstd[:, 0:n], vec[:, GAMMA, k0:k0 + n], ALU.mult).then_inc(s_gain, 1)
                dve.wait_ge(s_gain, s + 1)
                for k in range(n):
                    nc.vector.tensor_scalar(src[:, k, :], src[:, k, :], mean[:, k:k + 1], gain[:, k:k + 1],
                                            ALU.subtract, ALU.mult).then_inc(s_y, 1)

            def split_x(b, p, chunk, src):
                dve.wait_ge(s_xhi, KC * b + chunk + 1)
                nc.vector.scalar_tensor_tensor(out=xn_lo[p][:, chunk, :], in0=src,
                                               scalar=vec[:, BETA, chunk:chunk + 1],
                                               in1=xn_hi[p][:, chunk, :].bitcast(F32), op0=ALU.add,
                                               op1=ALU.subtract).then_inc(s_xlo, 1)

            def add_kdot(b, chunk, src):
                if chunk == 0:
                    nc.vector.tensor_scalar(kdot[:], src, k_row[:, 0:1], k_const[:],
                                            ALU.mult, ALU.add).then_inc(s_kdot, 1)
                else:
                    dve.wait_ge(s_kdot, KC * b + chunk)
                    nc.vector.scalar_tensor_tensor(out=kdot[:], in0=src,
                                                   scalar=k_row[:, chunk:chunk + 1], in1=kdot[:], op0=ALU.mult,
                                                   op1=ALU.add).then_inc(s_kdot, 1)

            def partial_sums(n, src, width):
                nc.vector.tensor_reduce(kdot_q[:, 0:width], src.rearrange("p (c r) -> p c r", r=Q), AX.X, ALU.add,
                                        apply_transpose=True).then_inc(s_colq, 1)
                dve.wait_ge(s_colq, n + 1)
                nc.vector.tensor_copy(col_hi[:, 0:width], kdot_q[:, 0:width]).then_inc(s_colhi, 1)
                dve.wait_ge(s_colhi, n + 1)
                nc.vector.tensor_tensor(col_lo[:, 0:width], kdot_q[:, 0:width], col_hi[:, 0:width].bitcast(F32),
                                        ALU.subtract).then_inc(s_collo, 1)

            def image_sums(b):
                dve.wait_ge(s_kdot, KC * b + KC)
                partial_sums(b + 1, kdot[:], N // Q)

            def read_columns(n, dst, width, slot=0):
                dve.wait_ge(s_col, n + 1)
                for q in range(NQ):
                    rows = slice(q * Q, (q + 1) * Q)
                    last = nc.vector.tensor_copy(dst[rows, :], ps_e[rows, slot, 0:NQ * width].rearrange(
                        "p (j q) -> p j q", q=NQ)[:, :, q])
                last.then_inc(s_colout, 1)

            def split_u(b, h, g, index):
                dve.wait_ge(s_uhi, 2 * KC * b + KC * h + g + 1)
                nc.vector.scalar_tensor_tensor(out=u_lo[:, g, :], in0=ps_a[:, index, :], scalar=u_bias[:, g:g + 1],
                                               in1=u_hi[:, g, :].bitcast(F32), op0=ALU.add,
                                               op1=ALU.subtract).then_inc(s_free, 1)

            def split_v(b, j, index):
                dve.wait_ge(s_vhi, NT * b + j + 1)
                nc.vector.tensor_tensor(v_lo[:, j, :], ps_a[:, index, :], v_hi[:, j, :].bitcast(F32),
                                        ALU.subtract).then_inc(s_free, 1)

            def shift(b, p, t):
                dve.wait_ge(s_e, NT * b + t + 1)
                nc.vector.tensor_reduce(row_max[:, t % 2:t % 2 + 1], ps_e[:, t % 2, :], AX.X, ALU.max).then_inc(s_max, 1)
                dve.wait_ge(s_max, NT * b + t + 1)
                nc.vector.scalar_tensor_tensor(out=neg_shift[:, t % 2:t % 2 + 1], in0=row_max[:, t % 2:t % 2 + 1],
                                               scalar=t_bias[:, p, t:t + 1], in1=t_bias[:, p, t:t + 1], op0=ALU.add,
                                               op1=ALU.subtract, reverse1=True).then_inc(s_shift, 1)

            def normalise(b, t):
                dve.wait_ge(s_exp, NT * b + t + 1)
                nc.vector.reciprocal(row_inv[:, t % 2:t % 2 + 1], row_sum[:, t % 2:t % 2 + 1]).then_inc(s_inv, 1)
                dve.wait_ge(s_inv, NT * b + t + 1)
                nc.vector.tensor_scalar(prob[:], prob[:], row_inv[:, t % 2:t % 2 + 1], None, ALU.mult).then_inc(s_p, 1)

            def transpose_blocks(b, t):
                if not (isinstance(b, int) and b == 0 and t == 0):
                    dve.wait_ge(s_spill, 16 * NQ * (NT * b + t))
                dve.wait_ge(s_p, NT * b + t + 1)
                nc.vector.transpose(blocks_out[:].rearrange("p q t a -> p t q a"),
                                    prob[:].rearrange("p (t q a) -> p t q a", q=NQ, a=Q)).then_inc(s_blocks, 1)

            def split_pt(b, t):
                dve.wait_ge(s_pthi, NT * b + t + 1)
                hi, lo = pt_of(b, t)
                nc.vector.tensor_tensor(lo.rearrange("p t (q a) -> p t q a", a=Q),
                                        blocks_in[:].rearrange("p q t a -> p t q a"),
                                        hi.rearrange("p t (q a) -> p t q a", a=Q).bitcast(F32),
                                        ALU.subtract).then_inc(s_ptlo, 1)

            def result(b, h, g, at, index):
                dve.wait_ge(s_acc, at + 1)
                dve.wait_ge(s_res[g % 2], 16 * (4 * b + 2 * h + g // 2 + 1))
                nc.vector.scalar_tensor_tensor(out=res[:, g % 2, :], in0=ps_a[:, index, :], scalar=o_bias[:, g:g + 1],
                                               in1=res[:, g % 2, :], op0=ALU.add, op1=ALU.add).then_inc(s_free, 1)

            def half(b, p, h, at, tiles, next_split, stats, u_of):
                s = set_of(*stats) if stats else None

                def softmax(n, split=None, moment=None):
                    bt, pt, t = tiles[n]
                    shift(bt, pt, t)
                    if split:
                        split_pt(*split)
                    if moment is not None:
                        pair_moments(*stats, moment)
                    normalise(bt, t)
                    return bt, t

                transpose_blocks(*softmax(0, split=next_split))
                last = softmax(1, moment=0 if stats else None)
                if stats:
                    pair_moments(*stats, 1)
                    dve.wait_ge(s_bn, 2 * s + 4)
                split_u(*u_of, 0, at("U", 1 - h, 0)[1])
                if stats:
                    aggregate(2)
                    split_mean(s, 2)
                transpose_blocks(*last)
                split_u(*u_of, 1, at("U", 1 - h, 1)[1])
                split_u(*u_of, 2, at("U", 1 - h, 2)[1])
                if h == 1:
                    read_columns(b + 2, t_bias[:, 1 - p, :], NT)
                if stats:
                    spread(s, 2, *at("S1", h))
                split_u(*u_of, 3, at("U", 1 - h, 3)[1])
                split_pt(tiles[0][0], tiles[0][2])
                transpose_blocks(*softmax(2, split=(tiles[1][0], tiles[1][2])))
                if stats:
                    gathered(var, 2, *at("S2", h))
                transpose_blocks(*softmax(3))
                if stats:
                    bs, pair = stats
                    ps = (1 - p) if h == 0 else p
                    centre(s, 2, 2 * pair, x_in)
                    split_x(bs, ps, 2 * pair, x_in[:, 0, :])
                for g in range(KC):
                    result(b, h, g, *at("O", h, g))
                    if stats and g == 0:
                        add_kdot(bs, 2 * pair, x_in[:, 0, :])
                        split_x(bs, ps, 2 * pair + 1, x_in[:, 1, :])
                    if stats and g == 1:
                        add_kdot(bs, 2 * pair + 1, x_in[:, 1, :])
                    if stats and g == 2 and pair == 1:
                        image_sums(bs)
                split_pt(tiles[2][0], tiles[2][2])

            def body(b, p, has_next2):
                at = turns(b, has_next2)
                half(b, p, 0, at, [(b, p, t) for t in (2, 3, 4, 5)], None, (b + 1, 1), (b, 1))
                half(b, p, 1, at, [(b, p, 6), (b, p, 7), (b + 1, 1 - p, 0), (b + 1, 1 - p, 1)], (b, 5),
                     (b + 2, 0) if has_next2 else None, (b + 1, 0))
                for j in range(NT):
                    split_v(b + 1, j, at("V", j)[1])
                    if j == 1:
                        split_pt(b + 1, 1)

            def last_body(b, p):
                at = turns(b)

                def softmax(t):
                    shift(b, p, t)
                    if t >= 6:
                        split_pt(b, t - 2)
                    normalise(b, t)
                    transpose_blocks(b, t)

                softmax(2)
                softmax(3)
                for g in range(KC):
                    if g == KC - 1:
                        split_pt(b, 2)
                    split_u(b, 1, g, at("U", 1, g)[1])
                split_pt(b, 3)
                for t in range(4, NT):
                    softmax(t)
                split_pt(b, 6)
                for g in range(KC):
                    result(b, 0, g, *at("O", 0, g))
                    if g == 1:
                        split_pt(b, 7)
                for g in range(KC):
                    result(b, 1, g, *at("O", 1, g))

            def split_weight(dst_hi, dst_lo, g, scale, n, at, index):
                dve.wait_ge(s_whi, n + 1)
                nc.vector.scalar_tensor_tensor(out=dst_lo[:, g, :], in0=ps_a[:, index, :], scalar=scale,
                                               in1=dst_hi[:, g, :].bitcast(F32), op0=ALU.mult,
                                               op1=ALU.subtract).then_inc(s_free, 1)

            def bias_product(which, weight, column, k, before):
                if k == 0:
                    nc.vector.tensor_scalar(bias_dot[:, which, :], weight[:, 0, :], vec[:, column, 0:1], None,
                                            ALU.mult).then_inc(s_bdot, 1)
                else:
                    dve.wait_ge(s_bdot, before)
                    nc.vector.scalar_tensor_tensor(out=bias_dot[:, which, :], in0=weight[:, k, :],
                                                   scalar=vec[:, column, k:k + 1], in1=bias_dot[:, which, :],
                                                   op0=ALU.mult, op1=ALU.add).then_inc(s_bdot, 1)

            dve.wait_ge(s_vec, 16)
            for k in range(KC):
                dve.wait_ge(s_wk[k], 16)
                bias_product(0, w_k, BQ, k, 2 * k - 1)
                dve.wait_ge(s_wq[k], 16)
                bias_product(1, w_q, BK, k, 2 * k)
            for k in range(KC):
                dve.wait_ge(s_x0[k], 16)
                moments(x_0[:, k, :], k)
            dve.wait_ge(s_bn, KC)
            aggregate(KC)
            split_mean(0, KC)
            for g in range(KC):
                split_weight(g_hi, g_lo, g, SCALE, g, *early_turn("G", g))
            spread(0, KC, *early_turn("S1", 0))
            dve.wait_ge(s_wpt, 16)
            for k in range(KC):
                bias_product(2, w_pt, BV, k, 2 * KC + k)
            split_weight(m_hi, m_lo, 0, 1.0, KC, *early_turn("M", 0))
            gathered(var, KC, *early_turn("S2", 0))
            dve.wait_ge(s_bdot, 3 * KC)
            partial_sums(0, bias_dot[:].rearrange("p w c -> p (w c)"), 3 * C // Q)
            centre(0, KC, 0, x_0)
            split_x(0, 0, 0, x_0[:, 0, :])
            split_x(0, 0, 1, x_0[:, 1, :])
            split_x(0, 0, 2, x_0[:, 2, :])
            split_x(0, 0, 3, x_0[:, 3, :])
            split_weight(m_hi, m_lo, 1, 1.0, KC + 1, *early_turn("M", 1))
            split_weight(m_hi, m_lo, 2, 1.0, KC + 2, *early_turn("M", 2))
            split_weight(m_hi, m_lo, 3, 1.0, KC + 3, *early_turn("M", 3))
            read_columns(0, columns[:].rearrange("p w k -> p (w k)"), 3 * KC)
            dve.wait_ge(s_colout, 1)
            nc.vector.tensor_scalar(k_row[:], columns[:, 1, :], SCALE, None, ALU.mult).then_inc(s_bias, 1)
            nc.vector.tensor_scalar(u_bias[:], columns[:, 0, :], SCALE, None, ALU.mult).then_inc(s_bias, 1)
            nc.vector.tensor_tensor(o_bias[:], columns[:, 2, :], vec[:, BP, :], ALU.add).then_inc(s_bias, 1)
            nc.vector.tensor_tensor(k_tmp[:, 0, :], vec[:, BQ, :], vec[:, BK, :], ALU.mult).then_inc(s_bias, 1)
            dve.wait_ge(s_bias, 1)
            nc.vector.tensor_tensor(k_tmp[:, 1, :], k_row[:], vec[:, BETA, :], ALU.mult).then_inc(s_bias, 1)
            dve.wait_ge(s_bias, 5)
            nc.vector.tensor_reduce(k_sum[:], k_tmp[:], AX.X, ALU.add).then_inc(s_bias, 1)
            dve.wait_ge(s_bias, 6)
            nc.vector.scalar_tensor_tensor(out=k_const[:], in0=k_sum[:, 0:1], scalar=SCALE, in1=k_sum[:, 1:2],
                                           op0=ALU.mult, op1=ALU.add).then_inc(s_bias, 1)
            dve.wait_ge(s_bias, 7)
            add_kdot(0, 0, x_0[:, 0, :])
            split_u(0, 0, 0, early_turn("U", 0)[1])
            add_kdot(0, 1, x_0[:, 1, :])
            add_kdot(0, 2, x_0[:, 2, :])
            split_u(0, 0, 1, early_turn("U", 1)[1])
            add_kdot(0, 3, x_0[:, 3, :])
            image_sums(0)
            split_u(0, 0, 2, early_turn("U", 2)[1])
            split_u(0, 0, 3, early_turn("U", 3)[1])
            for j in range(2):
                pair_moments(1, 0, j)
            dve.wait_ge(s_bn, KC + 2)
            read_columns(1, t_bias[:, 0, :], NT, slot=1)
            aggregate(2)
            split_mean(1, 2)
            for t in range(2):
                shift(0, 0, t)
                normalise(0, t)
                transpose_blocks(0, t)
            for j in range(NT):
                split_v(0, j, early_turn("V", j)[1])
                if j == 2:
                    spread(1, 2, *early_turn("S1", 1))
                    split_pt(0, 0)
                if j == 5:
                    gathered(var, 2, *early_turn("S2", 1))
                if j == 6:
                    centre(1, 2, 0, x_in)
                    split_pt(0, 1)
            for j in range(2):
                split_x(1, 1, j, x_in[:, j, :])
                add_kdot(1, j, x_in[:, j, :])
            with nc.vector.Fori(0, B // 2 - 1) as i:
                for p in range(2):
                    body(2 * i + p, p, True)
            body(B - 2, 0, False)
            last_body(B - 1, 1)


def kernel(**inputs):
    import concourse.bacc as bacc
    from concourse.bass_utils import run_bass_kernel_spmd

    x = np.ascontiguousarray(inputs["x"])
    b, c, h, w = x.shape
    names = ("gn_gamma", "gn_beta", "bq", "bk", "bv", "bp")
    columns = [np.asarray(inputs["L0_conv_" + n]).reshape(-1, 128).T for n in names]
    arrays = {
        "x": x.reshape(b, c, h * w),
        "wq": np.ascontiguousarray(inputs["L0_conv_wq"]),
        "wk": np.ascontiguousarray(inputs["L0_conv_wk"]),
        "wv": np.ascontiguousarray(inputs["L0_conv_wv"]),
        "wp_t": np.ascontiguousarray(np.asarray(inputs["L0_conv_wp"]).T),
        "vecs": np.ascontiguousarray(np.stack(columns, axis=1)),
    }
    nc = bacc.Bacc("TRN2", target_bir_lowering=False, num_devices=1)
    args = [nc.dram_tensor(n, a.shape, mybir.dt.from_np(a.dtype), kind="ExternalInput").ap() for n, a in arrays.items()]
    out = nc.dram_tensor("out", (b, c, h * w), F32, kind="ExternalOutput").ap()
    scratch = nc.dram_tensor("scratch", (h * w // 128, 4, 32, 4, h * w // 4), F32, kind="Internal").ap()
    build(nc, *args, scratch, out)
    result = run_bass_kernel_spmd(nc, [arrays], core_ids=[0])
    return result.results[0]["out"].reshape(b, c, h, w)
```
